# Optimizing a Trainium2 kernel written in Bass

```python
import numpy as np
import jax
import jax.numpy as jnp

def _softmax(x, axis=-1):
    return jax.nn.softmax(x, axis=axis)

def _gelu(x):
    return jax.nn.gelu(x, approximate=True)

def _silu(x):
    return jax.nn.silu(x)

def _sigmoid(x):
    return jax.nn.sigmoid(x)

def _layernorm(x, axis=-1, eps=1e-05):
    m = jnp.mean(x, axis=axis, keepdims=True)
    v = jnp.var(x, axis=axis, keepdims=True)
    return (x - m) / jnp.sqrt(v + eps)

def _scatter_add(tgt, idx, src, axis=0):
    return tgt.at[idx].add(src)

def _segment_sum(src, seg, n):
    return jax.ops.segment_sum(src, seg, n)
kernel_name = 'mk_vit_tower_postln_d2_tok_img1024_r4_5b4233'

def setup_inputs(seed: int=0):
    np.random.seed(seed)
    _w = jnp.asarray

    def _rec_inputs():
        import jax
        import jax.numpy as jnp
        _rk = jax.random.key(seed)
        x = -0.000356955 + 1 * jax.random.normal(jax.random.fold_in(_rk, 1), (64, 3, 224, 224), jnp.float32)
        return x
    x = _rec_inputs()

    def _L0_tok_setup():
        import jax, jax.numpy as jnp
        import numpy as np
        PH, PW = (16, 16)
        key = jax.random.key(seed)
        k1, k2 = jax.random.split(key)
        B, C, H, W_ = (128, 3, 224, 224)
        embed_dim = 256
        patch_dim = C * PH * PW
        x = jax.random.normal(k1, (B, C, H, W_), dtype=jnp.float32)
        W = jax.random.normal(k2, (embed_dim, patch_dim), dtype=jnp.float32) * 0.02
        b = jnp.zeros((embed_dim,), dtype=jnp.float32)
        return {'x': x, 'W': W, 'b': b}
    _L0_tok_all = _L0_tok_setup()
    _L0_tok_in = {k: v for k, v in _L0_tok_all.items() if k in ('W', 'b')}
    del _L0_tok_all

    def _L0_attn_setup():
        import jax, jax.numpy as jnp
        import numpy as np
        B, L, D_MODEL = (2, 256, 256)
        D_STATE, D_CONV, EXPAND = (16, 4, 2)
        D_INNER = D_MODEL * EXPAND
        LN_EPS = 1e-05

        def _forward(x, in_proj_w, conv_w, conv_b, x_proj_w, A_log, D_param, dt_w, dt_b, out_w, ln_g, ln_b):
            Lq = x.shape[1]
            xz = jnp.einsum('bld,ed->ble', x, in_proj_w)
            xb, z = (xz[..., :D_INNER], xz[..., D_INNER:])
            xpad = jnp.pad(xb, ((0, 0), (D_CONV - 1, 0), (0, 0)))
            xc = conv_b
            for k in range(D_CONV):
                xc = xc + xpad[:, k:k + Lq, :] * conv_w[:, k]
            xb = jax.nn.silu(xc)
            proj = jnp.einsum('bld,ed->ble', xb, x_proj_w)
            dt_in = proj[..., :1]
            Bp = proj[..., 1:1 + D_STATE]
            Cp = proj[..., 1 + D_STATE:]
            dt = jax.nn.softplus(dt_in * dt_w[:, 0] + dt_b)
            A = -jnp.exp(A_log)
            dA = jnp.exp(dt[..., None] * A)
            x_scaled = (xb * dt)[..., None] * Bp[..., None, :]

            def comb(a, b):
                return (a[0] * b[0], b[0] * a[1] + b[1])
            _, h = jax.lax.associative_scan(comb, (dA, x_scaled), axis=1)
            y = jnp.einsum('bldn,bln->bld', h, Cp) + xb * D_param
            mu = jnp.mean(y, axis=-1, keepdims=True)
            var = jnp.var(y, axis=-1, keepdims=True)
            y = (y - mu) / jnp.sqrt(var + LN_EPS) * ln_g + ln_b
            y = y * jax.nn.silu(z)
            return jnp.einsum('bld,ed->ble', y, out_w)
        key = jax.random.key(seed)
        ks = jax.random.split(key, 6)
        g = lambda k, shape, scale: jax.random.normal(k, shape, jnp.float32) * scale
        x = jax.random.normal(ks[0], (B, L, D_MODEL), jnp.float32)
        in_proj_w = g(ks[1], (2 * D_INNER, D_MODEL), D_MODEL ** (-0.5))
        conv_w = g(ks[2], (D_INNER, D_CONV), D_CONV ** (-0.5))
        conv_b = jnp.zeros((D_INNER,), jnp.float32)
        x_proj_w = g(ks[3], (2 * D_STATE + 1, D_INNER), D_INNER ** (-0.5))
        A_log = jnp.tile(jnp.log(jnp.arange(1, D_STATE + 1, dtype=jnp.float32)), (D_INNER, 1))
        D_param = jnp.ones((D_INNER,), jnp.float32)
        dt_w = g(ks[4], (D_INNER, 1), 1.0)
        dt_b = jnp.full((D_INNER,), -4.0, jnp.float32)
        out_w = g(ks[5], (D_MODEL, D_INNER), D_INNER ** (-0.5))
        ln_g = jnp.ones((D_INNER,), jnp.float32)
        ln_b = jnp.zeros((D_INNER,), jnp.float32)
        return dict(x=x, in_proj_w=in_proj_w, conv_w=conv_w, conv_b=conv_b, x_proj_w=x_proj_w, A_log=A_log, D_param=D_param, dt_w=dt_w, dt_b=dt_b, out_w=out_w, ln_g=ln_g, ln_b=ln_b)
    _L0_attn_all = _L0_attn_setup()
    _L0_attn_in = {k: v for k, v in _L0_attn_all.items() if k in ('in_proj_w', 'conv_w', 'conv_b', 'x_proj_w', 'A_log', 'D_param', 'dt_w', 'dt_b', 'out_w', 'ln_g', 'ln_b')}
    del _L0_attn_all

    def _L0_ffn_setup():
        import jax, jax.numpy as jnp
        import numpy as np
        DIM = 256

        def _reference_tuple_inner(x, W_r, W_k, W_v, mu_r, mu_k):
            B, T, C = x.shape
            x_prev = jnp.concatenate([jnp.zeros((B, 1, C), x.dtype), x[:, :-1, :]], axis=1)
            xr = mu_r * x + (1.0 - mu_r) * x_prev
            xk = mu_k * x + (1.0 - mu_k) * x_prev
            r = jax.nn.sigmoid(jnp.einsum('btc,dc->btd', xr, W_r))
            k = jnp.einsum('btc,dc->btd', xk, W_k)
            k_act = jnp.square(jax.nn.relu(k))
            out = r * jnp.einsum('btc,dc->btd', k_act, W_v)
            new_state = x[:, -1, :]
            return (out, new_state)
        key = jax.random.key(seed)
        ks = jax.random.split(key, 6)
        B, T, C = (8, 512, DIM)
        x = jax.random.normal(ks[0], (B, T, C), dtype=jnp.float32)
        s = 1.0 / np.sqrt(C)
        W_r = jax.random.uniform(ks[1], (C, C), jnp.float32, -s, s)
        W_k = jax.random.uniform(ks[2], (C, C), jnp.float32, -s, s)
        W_v = jax.random.uniform(ks[3], (C, C), jnp.float32, -s, s)
        mu_r = jax.random.uniform(ks[4], (C,), jnp.float32)
        mu_k = jax.random.uniform(ks[5], (C,), jnp.float32)
        return {'x': x, 'W_r': W_r, 'W_k': W_k, 'W_v': W_v, 'mu_r': mu_r, 'mu_k': mu_k}
    _L0_ffn_all = _L0_ffn_setup()
    _L0_ffn_in = {k: v for k, v in _L0_ffn_all.items() if k in ('W_r', 'W_k', 'W_v', 'mu_r', 'mu_k')}
    del _L0_ffn_all

    def _L1_attn_setup():
        import jax, jax.numpy as jnp
        import numpy as np
        import math
        HID_DIM = 256
        NUM_HEADS = 8
        QK_DIM = HID_DIM // 8
        key = jax.random.key(seed)
        ks = jax.random.split(key, 7)
        B, M, C = (4, 512, HID_DIM)
        gain = math.sqrt(2.0)

        def xavier(k, fan_in, fan_out):
            std = gain * math.sqrt(2.0 / (fan_in + fan_out))
            a = math.sqrt(3.0) * std
            return jax.random.uniform(k, (fan_out, fan_in), jnp.float32, -a, a)
        x = jax.random.normal(ks[0], (B, M, C), jnp.float32)
        Wq = xavier(ks[1], C, QK_DIM)
        Wk = xavier(ks[2], C, QK_DIM)
        Wv = xavier(ks[3], C, C)
        bq = jnp.zeros((QK_DIM,), jnp.float32)
        bk = jnp.zeros((QK_DIM,), jnp.float32)
        bv = jnp.zeros((C,), jnp.float32)
        gamma = jnp.zeros((1,), jnp.float32)
        return {'x': x, 'Wq': Wq, 'bq': bq, 'Wk': Wk, 'bk': bk, 'Wv': Wv, 'bv': bv, 'gamma': gamma}
    _L1_attn_all = _L1_attn_setup()
    _L1_attn_in = {k: v for k, v in _L1_attn_all.items() if k in ('Wq', 'bq', 'Wk', 'bk', 'Wv', 'bv', 'gamma')}
    del _L1_attn_all

    def _L1_ffn_setup():
        import jax, jax.numpy as jnp
        import numpy as np
        IN_DIM = 256
        OUT_DIM = 256
        NUM_EXPERTS = 8
        TOP_K = 2
        key = jax.random.key(seed)
        ks = jax.random.split(key, 5)
        s = 1.0 / np.sqrt(IN_DIM)
        x = jax.random.normal(ks[0], (4, 512, IN_DIM), dtype=jnp.float32)
        Wg = jax.random.uniform(ks[1], (IN_DIM, NUM_EXPERTS), jnp.float32, -s, s)
        bg = jnp.zeros((NUM_EXPERTS,), jnp.float32)
        We = jax.random.uniform(ks[2], (NUM_EXPERTS, OUT_DIM, IN_DIM), jnp.float32, -s, s)
        be = jax.random.uniform(ks[3], (NUM_EXPERTS, OUT_DIM), jnp.float32, -s, s)
        return {'x': x, 'Wg': Wg, 'bg': bg, 'We': We, 'be': be}
    _L1_ffn_all = _L1_ffn_setup()
    _L1_ffn_in = {k: v for k, v in _L1_ffn_all.items() if k in ('Wg', 'bg', 'We', 'be')}
    del _L1_ffn_all
    return {'x': x, 'L0_tok_W': _L0_tok_in['W'], 'L0_tok_b': _L0_tok_in['b'], 'L0_attn_in_proj_w': _L0_attn_in['in_proj_w'], 'L0_attn_conv_w': _L0_attn_in['conv_w'], 'L0_attn_conv_b': _L0_attn_in['conv_b'], 'L0_attn_x_proj_w': _L0_attn_in['x_proj_w'], 'L0_attn_A_log': _L0_attn_in['A_log'], 'L0_attn_D_param': _L0_attn_in['D_param'], 'L0_attn_dt_w': _L0_attn_in['dt_w'], 'L0_attn_dt_b': _L0_attn_in['dt_b'], 'L0_attn_out_w': _L0_attn_in['out_w'], 'L0_attn_ln_g': _L0_attn_in['ln_g'], 'L0_attn_ln_b': _L0_attn_in['ln_b'], 'L0_ffn_W_r': _L0_ffn_in['W_r'], 'L0_ffn_W_k': _L0_ffn_in['W_k'], 'L0_ffn_W_v': _L0_ffn_in['W_v'], 'L0_ffn_mu_r': _L0_ffn_in['mu_r'], 'L0_ffn_mu_k': _L0_ffn_in['mu_k'], 'L1_attn_Wq': _L1_attn_in['Wq'], 'L1_attn_bq': _L1_attn_in['bq'], 'L1_attn_Wk': _L1_attn_in['Wk'], 'L1_attn_bk': _L1_attn_in['bk'], 'L1_attn_Wv': _L1_attn_in['Wv'], 'L1_attn_bv': _L1_attn_in['bv'], 'L1_attn_gamma': _L1_attn_in['gamma'], 'L1_ffn_Wg': _L1_ffn_in['Wg'], 'L1_ffn_bg': _L1_ffn_in['bg'], 'L1_ffn_We': _L1_ffn_in['We'], 'L1_ffn_be': _L1_ffn_in['be']}

def reference(x, L0_tok_W, L0_tok_b, L0_attn_in_proj_w, L0_attn_conv_w, L0_attn_conv_b, L0_attn_x_proj_w, L0_attn_A_log, L0_attn_D_param, L0_attn_dt_w, L0_attn_dt_b, L0_attn_out_w, L0_attn_ln_g, L0_attn_ln_b, L0_ffn_W_r, L0_ffn_W_k, L0_ffn_W_v, L0_ffn_mu_r, L0_ffn_mu_k, L1_attn_Wq, L1_attn_bq, L1_attn_Wk, L1_attn_bk, L1_attn_Wv, L1_attn_bv, L1_attn_gamma, L1_ffn_Wg, L1_ffn_bg, L1_ffn_We, L1_ffn_be):
    import jax
    import jax.numpy as jnp

    def _L0_tok_ref(x, W, b):
        import jax, jax.numpy as jnp
        import numpy as np
        PH, PW = (16, 16)
        B, C, H, Wd = x.shape
        nh, nw = (H // PH, Wd // PW)
        p = x.reshape(B, C, nh, PH, nw, PW).transpose(0, 2, 4, 1, 3, 5)
        p = p.reshape(B, nh * nw, C * PH * PW)
        return jnp.einsum('bnp,dp->bnd', p, W) + b

    def _L0_attn_ref(x, in_proj_w, conv_w, conv_b, x_proj_w, A_log, D_param, dt_w, dt_b, out_w, ln_g, ln_b):
        import jax, jax.numpy as jnp
        import numpy as np
        B, L, D_MODEL = (2, 256, 256)
        D_STATE, D_CONV, EXPAND = (16, 4, 2)
        D_INNER = D_MODEL * EXPAND
        LN_EPS = 1e-05

        def _forward(x, in_proj_w, conv_w, conv_b, x_proj_w, A_log, D_param, dt_w, dt_b, out_w, ln_g, ln_b):
            Lq = x.shape[1]
            xz = jnp.einsum('bld,ed->ble', x, in_proj_w)
            xb, z = (xz[..., :D_INNER], xz[..., D_INNER:])
            xpad = jnp.pad(xb, ((0, 0), (D_CONV - 1, 0), (0, 0)))
            xc = conv_b
            for k in range(D_CONV):
                xc = xc + xpad[:, k:k + Lq, :] * conv_w[:, k]
            xb = jax.nn.silu(xc)
            proj = jnp.einsum('bld,ed->ble', xb, x_proj_w)
            dt_in = proj[..., :1]
            Bp = proj[..., 1:1 + D_STATE]
            Cp = proj[..., 1 + D_STATE:]
            dt = jax.nn.softplus(dt_in * dt_w[:, 0] + dt_b)
            A = -jnp.exp(A_log)
            dA = jnp.exp(dt[..., None] * A)
            x_scaled = (xb * dt)[..., None] * Bp[..., None, :]

            def comb(a, b):
                return (a[0] * b[0], b[0] * a[1] + b[1])
            _, h = jax.lax.associative_scan(comb, (dA, x_scaled), axis=1)
            y = jnp.einsum('bldn,bln->bld', h, Cp) + xb * D_param
            mu = jnp.mean(y, axis=-1, keepdims=True)
            var = jnp.var(y, axis=-1, keepdims=True)
            y = (y - mu) / jnp.sqrt(var + LN_EPS) * ln_g + ln_b
            y = y * jax.nn.silu(z)
            return jnp.einsum('bld,ed->ble', y, out_w)
        return _forward(x, in_proj_w, conv_w, conv_b, x_proj_w, A_log, D_param, dt_w, dt_b, out_w, ln_g, ln_b)

    def _L0_ffn_ref(x, W_r, W_k, W_v, mu_r, mu_k):
        import jax, jax.numpy as jnp
        import numpy as np
        DIM = 256

        def _reference_tuple_inner(x, W_r, W_k, W_v, mu_r, mu_k):
            B, T, C = x.shape
            x_prev = jnp.concatenate([jnp.zeros((B, 1, C), x.dtype), x[:, :-1, :]], axis=1)
            xr = mu_r * x + (1.0 - mu_r) * x_prev
            xk = mu_k * x + (1.0 - mu_k) * x_prev
            r = jax.nn.sigmoid(jnp.einsum('btc,dc->btd', xr, W_r))
            k = jnp.einsum('btc,dc->btd', xk, W_k)
            k_act = jnp.square(jax.nn.relu(k))
            out = r * jnp.einsum('btc,dc->btd', k_act, W_v)
            new_state = x[:, -1, :]
            return (out, new_state)
        return _reference_tuple_inner(x, W_r, W_k, W_v, mu_r, mu_k)[0]

    def _L1_attn_ref(x, Wq, bq, Wk, bk, Wv, bv, gamma):
        import jax, jax.numpy as jnp
        import numpy as np
        import math
        HID_DIM = 256
        NUM_HEADS = 8
        QK_DIM = HID_DIM // 8
        B, M, C = x.shape
        H = NUM_HEADS
        dqk = QK_DIM // H
        dv = C // H
        q = (x @ Wq.T + bq).reshape(B, M, H, dqk)
        k = (x @ Wk.T + bk).reshape(B, M, H, dqk)
        v = (x @ Wv.T + bv).reshape(B, M, H, dv)
        scores = jnp.einsum('bmhd,bnhd->bhmn', q, k) / math.sqrt(dqk)
        scores = jnp.where(scores >= 0, scores, 0.2 * scores)
        beta = jax.nn.softmax(scores, axis=-1)
        out = jnp.einsum('bhmn,bnhd->bmhd', beta, v).reshape(B, M, C)
        return gamma * out + x

    def _L1_ffn_ref(x, Wg, bg, We, be):
        import jax, jax.numpy as jnp
        import numpy as np
        IN_DIM = 256
        OUT_DIM = 256
        NUM_EXPERTS = 8
        TOP_K = 2
        gate = jax.nn.softmax(x @ Wg + bg, axis=-1)
        topk_vals, topk_idx = jax.lax.top_k(gate, TOP_K)
        onehot = jax.nn.one_hot(topk_idx, NUM_EXPERTS, dtype=gate.dtype)
        gate_sparse = jnp.einsum('bsk,bske->bse', topk_vals, onehot)
        gate_sparse = gate_sparse / jnp.sum(gate_sparse, axis=-1, keepdims=True)
        y = jnp.einsum('bsi,eoi->bseo', x, We) + be[None, None, :, :].transpose(0, 1, 2, 3)
        out = jnp.einsum('bseo,bse->bso', y, gate_sparse)
        return out
    h = _L0_tok_ref(x, L0_tok_W, L0_tok_b)
    h = _layernorm(h + _L0_attn_ref(h, L0_attn_in_proj_w, L0_attn_conv_w, L0_attn_conv_b, L0_attn_x_proj_w, L0_attn_A_log, L0_attn_D_param, L0_attn_dt_w, L0_attn_dt_b, L0_attn_out_w, L0_attn_ln_g, L0_attn_ln_b), axis=-1)
    h = _layernorm(h + _L0_ffn_ref(h, L0_ffn_W_r, L0_ffn_W_k, L0_ffn_W_v, L0_ffn_mu_r, L0_ffn_mu_k), axis=-1)
    h = _layernorm(h + _L1_attn_ref(h, L1_attn_Wq, L1_attn_bq, L1_attn_Wk, L1_attn_bk, L1_attn_Wv, L1_attn_bv, L1_attn_gamma), axis=-1)
    h = _layernorm(h + _L1_ffn_ref(h, L1_ffn_Wg, L1_ffn_bg, L1_ffn_We, L1_ffn_be), axis=-1)
    return h

_drawn_inputs = setup_inputs


def setup_inputs(seed=0):
    import zlib

    import numpy as np

    out = dict(_drawn_inputs(seed))
    spreads = {'L0_tok_b': (0.0, 0.1),
     'L0_attn_conv_b': (0.0, 0.1),
     'L0_attn_D_param': (1.0, 0.2),
     'L0_attn_dt_b': (-4.0, 0.6),
     'L0_attn_ln_g': (1.0, 0.2),
     'L0_attn_ln_b': (0.0, 0.1),
     'L1_attn_bq': (0.0, 0.1),
     'L1_attn_bk': (0.0, 0.1),
     'L1_attn_bv': (0.0, 0.1),
     'L1_ffn_bg': (0.0, 0.1)}
    factors = {'L0_attn_dt_w': 3.523}
    for name, (base, spread) in spreads.items():
        noise = np.random.default_rng([zlib.crc32(name.encode()), seed]).standard_normal(out[name].shape)
        drawn = base * np.exp(spread * noise) if base else spread * noise
        out[name] = jnp.asarray(drawn.astype(out[name].dtype))
    for name, factor in factors.items():
        out[name] = (out[name] * factor).astype(out[name].dtype)
    return out
```

```python
from contextlib import ExitStack

import concourse.bass as bass
from concourse import mybir

F32 = mybir.dt.float32
BF16 = mybir.dt.bfloat16
ALU = mybir.AluOpType
ACT = mybir.ActivationFunctionType
AX_X = mybir.AxisListType.X

P = 128
IMAGES = 64
COLORS = 3
SIDE = 14
PATCH = 16
WIDTH = SIDE * PATCH
T = SIDE * SIDE
BLK = 2
TB = T // BLK
D = 256
DC = D // P
INNER = 512
IC = INNER // P
STATES = 16
TAPS = 4
HALVES = 2
KP = COLORS * HALVES
CROWS = COLORS * SIDE
PROJ = 2 * STATES + 1
PARTS = 3
STK = PARTS * PROJ
NG = 4
GC = STATES // NG
GROUPS = IC * GC
RING = 4
DRING = 2
HEADS = 8
QK = D // HEADS
DV = D // HEADS
HU = 4
UNITS = BLK * (HEADS // HU)
EXPERTS = 8
LN_EPS = 1e-5
SLOPE = 0.2

U_PATCH = 0
PATCH_USES = ((0, 12), (12, 14), (14, 26), (26, 28))
U_EMBED = U_PATCH + len(PATCH_USES)
U_XB = U_EMBED + DC
U_Z = U_XB + 2
U_XPROJ = U_Z + 2
U_DT = U_XPROJ + 1
U_BC = U_DT + 1
BC_USES = 2 * STATES // 2
USES = U_BC + BC_USES
assert USES % 2 == 0

AT_PX = {0: 0, 2: 1}
AT_PATCH = {1: 0, 3: 1}
AT_EMBED, AT_XB, AT_CONV, AT_Z, AT_SILU, AT_XPROJ, AT_SPLIT, AT_DT, AT_SOFT, AT_U = 4, 5, 6, 6, 7, 8, 9, 10, 11, 12
AT_BC = {13: 0, 14: 1, 15: 2}
AT_YSTATS, AT_YNORM, AT_OUT, AT_LN1, AT_H1T, AT_RK, AT_VMM, AT_LN2, AT_H2T = 0, 1, 3, 4, 5, 7, 8, 9, 10
AT_QKV, AT_S0, AT_P0 = 12, 13, 14
AT_UNIT1 = 15
AT_PT = {0: 1, 2: 2, 4: 3}
AT_AVS = {1: 1, 3: 2}
AT_AV3, AT_H3T, AT_GATE, AT_WS = 5, 6, 7, 8
AT_MOE = {7: (0, 1), 8: (2,), 9: (3, 4), 10: (5, 6), 11: (7,)}
AT_ADD = {8: (0, 1), 9: (2, 3), 10: (4, 5), 11: (6, 7)}
AT_BE = 11
MOE_BANK = (2, 0, 2, 0, 1, 2, 0, 1)


def after(eng, sem, count):
    if isinstance(count, int) and count <= 0:
        return
    eng.wait_ge(sem, count)


def vit_tower(nc, x, w_tok, b_tok, w_in, conv_w, conv_b, w_xproj, a_log, d_par, dt_w, dt_b, w_out, ln_g, ln_b,
              w_r, w_k, w_v, mu_r, mu_k, w_q, b_q, w_kk, b_k, w_vv, b_v, gamma, w_g, b_g, w_e, b_e,
              ident, select, split_masks, head_mask, rank, out):
    with ExitStack() as ctx:
        def sb(name, shape, dt=F32):
            return ctx.enter_context(nc.sbuf_tensor(name, shape, dt))

        def psum(name, shape):
            return ctx.enter_context(nc.psum_tensor(name, shape, F32))

        def sem(name):
            return ctx.enter_context(nc.semaphore(name))

        wtok = sb("wtok", [P, KP, D])
        btok = sb("btok", [P, DC])
        win = sb("win", [P, DC, 2 * INNER])
        cw = sb("cw", [P, IC, TAPS])
        cb = sb("cb", [P, IC])
        wxp = sb("wxp", [P, IC, STK])
        negA = sb("negA", [P, IC, STATES])
        dpar = sb("dpar", [P, IC])
        dtw = sb("dtw", [P, IC])
        dtb = sb("dtb", [P, IC])
        wout = sb("wout", [P, IC, D])
        lng = sb("lng", [P, IC])
        lnb = sb("lnb", [P, IC])
        wr = sb("wr", [P, DC, D])
        wk = sb("wk", [P, DC, D])
        wv = sb("wv", [P, DC, D])
        mur = sb("mur", [P, DC])
        muk = sb("muk", [P, DC])
        omr = sb("omr", [P, DC])
        omk = sb("omk", [P, DC])
        wq = sb("wq", [P, DC, QK])
        bq = sb("bq", [QK, 1])
        wkk = sb("wkk", [P, DC, QK])
        bk = sb("bk", [QK, 1])
        wvv = sb("wvv", [P, DC, D])
        bv = sb("bv", [TB, D])
        gam = sb("gam", [TB, 1])
        wg = sb("wg", [P, DC, EXPERTS])
        bg = sb("bg", [TB, BLK, EXPERTS])
        we = sb("we", [P, DC, EXPERTS * D])
        be = sb("be", [EXPERTS, D])
        idn = sb("idn", [P, P])
        selF = sb("selF", [STK, PROJ])
        sel = sb("sel", [STK, PROJ], BF16)
        spl = sb("spl", [STK, 2])
        hm = sb("hm", [QK, HEADS])
        rk = sb("rk", [TB, BLK, EXPERTS])
        epsc = sb("epsc", [P, 1])

        xin = sb("xin", [CROWS, PATCH * WIDTH])
        px = sb("px", [CROWS, SIDE, PATCH // HALVES, PATCH])
        patT = sb("patT", [P, HALVES * SIDE, CROWS])
        hT = [sb(f"hT{i}", [P, DC, T]) for i in range(2)]
        xpad = sb("xpad", [P, IC, TAPS - 1 + T])
        xbs = sb("xbs", [P, IC, T])
        zs = [sb(f"zs{i}", [P, IC, T]) for i in range(2)]
        pj = sb("pj", [STK, T])
        pj1 = sb("pj1", [STK, T])
        hi1 = sb("hi1", [STK, T], BF16)
        hi2 = sb("hi2", [STK, T], BF16)
        stack = sb("stack", [STK, T], BF16)
        dtin = sb("dtin", [P, T])
        soft = sb("soft", [P, IC, T])
        dt_ = [sb(f"dt{i}", [P, IC, T]) for i in range(2)]
        u = [sb(f"u{i}", [P, IC, T]) for i in range(2)]
        xD = [sb(f"xD{i}", [P, IC, T]) for i in range(2)]
        Bb = sb("Bb", [P, STATES, T])
        Cb = sb("Cb", [P, STATES, T])
        dA = [sb(f"dA{i}", [P, NG, T]) for i in range(DRING)]
        X = [sb(f"X{i}", [P, NG, T]) for i in range(RING)]
        ysb = sb("ysb", [TB, BLK, INNER])
        y3 = sb("y3", [P, IC, T])
        h1 = sb("h1", [TB, BLK, D])
        h1T = sb("h1T", [P, DC, 1 + T])
        xr = sb("xr", [P, DC, T])
        xk = sb("xk", [P, DC, T])
        rs = sb("rs", [TB, BLK, D])
        ka = sb("ka", [P, DC, T])
        h2 = sb("h2", [TB, BLK, D])
        h2T = sb("h2T", [P, DC, T])
        qs = sb("qs", [QK, T])
        ks = sb("ks", [QK, T])
        qm = sb("qm", [QK, HEADS, T])
        vs = sb("vs", [TB, BLK, D])
        pr = sb("pr", [TB, HU, T])
        pT = sb("pT", [TB, 2, 2 * T])
        nmx = sb("nmx", [TB, HU])
        sums = sb("sums", [TB, HU])
        rg = sb("rg", [TB, HU])
        att = sb("att", [TB, BLK, D])
        h3 = sb("h3", [TB, BLK, D])
        h3T = sb("h3T", [P, DC, T])
        acc = sb("acc", [TB, BLK, D])
        ob = sb("ob", [TB, BLK, D])
        gl = sb("gl", [TB, BLK, EXPERTS])
        gw = sb("gw", [TB, BLK, EXPERTS])
        g2 = sb("g2", [TB, BLK, EXPERTS])
        oh1 = sb("oh1", [TB, BLK, EXPERTS])
        oh2 = sb("oh2", [TB, BLK, EXPERTS])
        gs = sb("gs", [TB, 6, BLK])
        wsT = sb("wsT", [EXPERTS, T])
        LN = ("y", "out", "ffn", "att", "moe")
        stat = {n: sb(f"stat_{n}", [TB, BLK, 6]) for n in LN}
        mv = {n: sb(f"mv_{n}", [TB, BLK, 2]) for n in LN}
        lnv = {n: sb(f"lnv_{n}", [TB, BLK]) for n in LN}
        rstd = {n: sb(f"rstd_{n}", [TB, BLK]) for n in LN}

        FB = psum("FB", [P, 2, 512])
        YB = psum("YB", [P, 512])
        AB = psum("AB", [P, 2, 512])
        BB = psum("BB", [P, 3, 512])

        x_landed = sem("x_landed")
        w_landed = sem("w_landed")
        out_landed = sem("out_landed")
        px_ready = sem("px_ready")
        f_filled = sem("f_filled")
        f_drained = sem("f_drained")
        const_ready = sem("const_ready")
        nega_exp = sem("nega_exp")
        zeros_ready = sem("zeros_ready")
        conv_step = sem("conv_step")
        silu_ready = sem("silu_ready")
        xD_ready = sem("xD_ready")
        split_step = sem("split_step")
        soft_step = sem("soft_step")
        lin_ready = sem("lin_ready")
        dt_ready = sem("dt_ready")
        u_ready = sem("u_ready")
        dA_ready = sem("dA_ready")
        xs_ready = sem("xs_ready")
        scan_done = sem("scan_done")
        prod_ready = sem("prod_ready")
        prod_used = sem("prod_used")
        y_drained = sem("y_drained")
        stats_step = {n: sem(f"stats_{n}") for n in LN}
        rstd_step = {n: sem(f"rstd_{n}") for n in LN}
        normed = {n: sem(f"normed_{n}") for n in LN}
        ynT_filled = sem("ynT_filled")
        yg_ready = sem("yg_ready")
        y3_ready = sem("y3_ready")
        out_filled = sem("out_filled")
        h1T_filled = sem("h1T_filled")
        h1T_ready = sem("h1T_ready")
        mix_step = sem("mix_step")
        r_filled = sem("r_filled")
        k_filled = sem("k_filled")
        r_ready = sem("r_ready")
        krelu_ready = sem("krelu_ready")
        ksq_ready = sem("ksq_ready")
        v_filled = sem("v_filled")
        ffn_step = sem("ffn_step")
        h2T_filled = sem("h2T_filled")
        h2T_ready = sem("h2T_ready")
        qk_filled = sem("qk_filled")
        vv_filled = sem("vv_filled")
        qk_ready = sem("qk_ready")
        qm_ready = sem("qm_ready")
        vv_ready = sem("vv_ready")
        s_filled = sem("s_filled")
        slope_ready = sem("slope_ready")
        leaky_ready = sem("leaky_ready")
        nmx_ready = sem("nmx_ready")
        pr_ready = sem("pr_ready")
        pT_filled = sem("pT_filled")
        pT_ready = sem("pT_ready")
        av_filled = sem("av_filled")
        av_step = sem("av_step")
        att_sum = sem("att_sum")
        h3T_filled = sem("h3T_filled")
        h3T_ready = sem("h3T_ready")
        gate_filled = sem("gate_filled")
        gate_step = sem("gate_step")
        gate_exp = sem("gate_exp")
        wsT_filled = sem("wsT_filled")
        wsT_ready = sem("wsT_ready")
        moe_filled = sem("moe_filled")
        moe_step = sem("moe_step")
        dve_past = sem("dve_past")
        pe_past = sem("pe_past")
        pool_past = sem("pool_past")
        GSTEPS = 20

        flat = x.rearrange("(b r) n -> b r n", r=CROWS)
        out_v = out.rearrange("(b k p) d -> b p k d", k=BLK, p=TB)
        loads = [(wtok, w_tok), (btok, b_tok), (win, w_in), (cw, conv_w), (cb, conv_b), (wxp, w_xproj),
                 (negA, a_log), (dpar, d_par), (dtw, dt_w), (dtb, dt_b), (wout, w_out), (lng, ln_g), (lnb, ln_b),
                 (wr, w_r), (wk, w_k), (wv, w_v), (mur, mu_r), (muk, mu_k), (wq, w_q), (bq, b_q), (wkk, w_kk),
                 (bk, b_k), (wvv, w_vv), (bv, b_v), (gam, gamma), (wg, w_g), (bg, b_g), (we, w_e), (be, b_e),
                 (idn, ident), (selF, select), (spl, split_masks), (hm, head_mask), (rk, rank)]
        W_ALL = 16 * len(loads)
        CONSTS = 5

        def schedule(body):
            body.prologue()
            body.step(0, 0, front=True, scan=True, a=False, b_head=False, b_rest=False)
            body.step(1, 1, front=True, scan=True, a=True, b_head=True, b_rest=False)
            with body.eng.Fori(1, IMAGES // 2 - 1) as pair:
                b = pair * 2
                body.step(b, 0, front=True, scan=True, a=True, b_head=True, b_rest=True)
                body.step(b + 1, 1, front=True, scan=True, a=True, b_head=True, b_rest=True)
            n = IMAGES
            body.step(n - 2, 0, front=True, scan=True, a=True, b_head=True, b_rest=True)
            body.step(n - 1, 1, front=False, scan=True, a=True, b_head=True, b_rest=True)
            body.step(n, 0, front=False, scan=False, a=True, b_head=True, b_rest=True)
            body.step(n + 1, 1, front=False, scan=False, a=False, b_head=False, b_rest=True)

        class Body:
            pass

        block = ctx.enter_context(nc.Block())

        @block.sync
        def _(sp):
            body = Body()
            body.eng = sp

            def load(s):
                if not (isinstance(s, int) and s == 0):
                    after(sp, px_ready, HALVES * s)
                src = flat[s, :, :] if isinstance(s, int) else flat[bass.ds(s, 1), :, :].rearrange("a r n -> (a r) n")
                sp.dma_start(xin[:], src).then_inc(x_landed, 16)

            def prologue():
                load(0)
                for dst, src in loads:
                    sp.dma_start(dst[:], src).then_inc(w_landed, 16)
                load(1)

            def step(b, par, front, scan, a, b_head, b_rest):
                if front and not (isinstance(b, int) and b + 2 >= IMAGES):
                    load(b + 2)
                if b_rest:
                    s = b - 2
                    after(sp, normed["moe"], BLK * (s + 1))
                    dst = out_v[s] if isinstance(s, int) else \
                        out_v[bass.ds(s, 1)].rearrange("a p k d -> (a p) k d")
                    sp.dma_start(dst, ob[:]).then_inc(out_landed, 16)

            body.prologue, body.step = prologue, step
            schedule(body)
            sp.wait_ge(out_landed, 16 * IMAGES)

        @block.gpsimd
        def _(pool):
            body = Body()
            body.eng = pool

            def prologue():
                nc.gpsimd.memset(xpad[:, :, 0:TAPS - 1], 0.0)
                nc.gpsimd.memset(h1T[:, :, 0:1], 0.0)
                nc.gpsimd.memset(epsc[:], LN_EPS)
                for i in range(DRING):
                    last = nc.gpsimd.memset(dA[i][:, :, 0:1], 0.0)
                last.then_inc(zeros_ready, 1)

            def step(b, par, front, scan, a, b_head, b_rest):
                for g in range(GROUPS):
                    if scan:
                        pool.wait_ge(scan_done, GROUPS * b + g + 1)
                        pool.wait_ge(f_drained, USES * b + U_BC + 4 * (g % GC) + 4)
                        t = X[g % RING]
                        n0 = NG * (g % GC)
                        nc.gpsimd.tensor_tensor(t[:], t[:], Cb[:, n0:n0 + NG, :], ALU.mult).then_inc(prod_ready, 1)
                    if front and g in AT_PX:
                        reorder(b + 1, AT_PX[g])
                    if front and g == AT_U:
                        s, q = b + 1, 1 - par
                        pool.wait_ge(dt_ready, s + 1)
                        pool.wait_ge(silu_ready, s + 1)
                        after(pool, xs_ready, GROUPS * (s - 1))
                        nc.gpsimd.tensor_tensor(u[q][:], dt_[q][:], xbs[:], ALU.mult).then_inc(u_ready, 1)
                    if a and g == AT_YNORM:
                        s, q = b - 1, 1 - par
                        pool.wait_ge(yg_ready, 2 * s + 2)
                        pool.wait_ge(f_drained, USES * s + U_XPROJ)
                        nc.gpsimd.tensor_tensor(y3[:], y3[:], zs[q][:], ALU.mult).then_inc(y3_ready, 1)
                    if a and g == AT_RK:
                        s = b - 1
                        pool.wait_ge(krelu_ready, s + 1)
                        nc.gpsimd.tensor_tensor(ka[:], ka[:], ka[:], ALU.mult).then_inc(ksq_ready, 1)

            def reorder(s, h):
                if h == 0:
                    pool.wait_ge(x_landed, 16 * (s + 1))
                after(pool, f_filled, USES * s + 2 if h else USES * (s - 1) + U_EMBED)
                pool.sem_inc(pool_past, 1)
                src = xin[:].rearrange("r (h p q w) -> r h q p w", h=HALVES, p=PATCH // HALVES, w=PATCH)
                nc.gpsimd.tensor_copy(px[:], src[:, h]).then_inc(px_ready, 1)

            def first():
                prologue()
                reorder(0, 0)
                reorder(0, 1)
                pool.wait_ge(dt_ready, 1)
                pool.wait_ge(silu_ready, 1)
                nc.gpsimd.tensor_tensor(u[0][:], dt_[0][:], xbs[:], ALU.mult).then_inc(u_ready, 1)

            body.prologue, body.step = first, step
            schedule(body)

        @block.tensor
        def _(pe):
            body = Body()
            body.eng = pe
            mm = nc.tensor.matmul

            def use(s, f):
                after(pe, f_drained, USES * s + f - 1)
                return FB[:, f % 2, :]

            def patches(s, h):
                pe.wait_ge(px_ready, HALVES * s + h + 1)
                for f in (2 * h, 2 * h + 1):
                    q0, q1 = PATCH_USES[f]
                    o = use(s, U_PATCH + f)
                    pe.sem_inc(pe_past, 1)
                    for q in range(q0, q1):
                        last = nc.tensor.transpose(o[:, (q - q0) * CROWS:(q - q0 + 1) * CROWS],
                                                   px[:, q % SIDE, :, :].rearrange("r p w -> r (p w)"),
                                                   idn[:CROWS, :CROWS])
                    last.then_inc(f_filled, 1)

            def embed(s):
                for m in range(DC):
                    o = use(s, U_EMBED + m)
                    after(pe, f_drained, USES * s + U_EMBED)
                    for k in range(KP):
                        c, half = k // HALVES, k % HALVES
                        rhs = patT[:, half * SIDE:(half + 1) * SIDE, c * SIDE:(c + 1) * SIDE].rearrange(
                            "p w h -> p h w")
                        last = mm(o[:, 0:T], lhsT=wtok[:, k, m * P:(m + 1) * P], rhs=rhs,
                                  start=(k == 0), stop=(k == KP - 1))
                    last.then_inc(f_filled, 1)

            def project_in(s, q, first_use, first_chunk):
                pe.wait_ge(f_drained, USES * s + U_XB)
                for f in range(2):
                    o = use(s, first_use + f)
                    for j in range(2):
                        m = first_chunk + 2 * f + j
                        for k in range(DC):
                            last = mm(o[:, j * T:(j + 1) * T], lhsT=win[:, k, m * P:(m + 1) * P],
                                      rhs=hT[q][:, k, :], start=(k == 0), stop=(k == DC - 1))
                    last.then_inc(f_filled, 1)

            def xproj(s):
                pe.wait_ge(silu_ready, s + 1)
                o = use(s, U_XPROJ)
                for k in range(IC):
                    last = mm(o[0:STK, 0:T], lhsT=wxp[:, k, :], rhs=xbs[:, k, :], start=(k == 0), stop=(k == IC - 1))
                last.then_inc(f_filled, 1)

            def spread(o, row):
                return mm(o, lhsT=sel[:, row:row + 1].broadcast_to([STK, P]), rhs=stack[:], start=True, stop=True)

            def dt_row(s):
                pe.wait_ge(split_step, 4 * s + 4)
                spread(use(s, U_DT)[:, 0:T], 0).then_inc(f_filled, 1)

            def spread_bc(s, ng):
                for i in range(4):
                    f = U_BC + 4 * ng + i
                    o = use(s, f)
                    row = 1 + STATES * (i // 2) + NG * ng + 2 * (i % 2)
                    spread(o[:, 0:T], row)
                    spread(o[:, T:2 * T], row + 1).then_inc(f_filled, 1)

            def sum_states(s, q, g):
                c = g // GC
                if g % GC == 0:
                    pe.wait_ge(xD_ready, s + 1)
                    after(pe, y_drained, IC * s + c)
                    for k in range(BLK):
                        mm(YB[0:TB, k * P:(k + 1) * P], lhsT=xD[q][:, c, k * TB:(k + 1) * TB], rhs=idn[:],
                           is_transpose=True, start=(k == 0), stop=False, skip_group_check=True)
                pe.wait_ge(prod_ready, GROUPS * s + g + 1)
                for j in range(NG):
                    for k in range(BLK):
                        last = mm(YB[0:TB, k * P:(k + 1) * P], lhsT=X[g % RING][:, j, k * TB:(k + 1) * TB],
                                  rhs=idn[:], is_transpose=True, start=False,
                                  stop=(g % GC == GC - 1 and j == NG - 1), skip_group_check=True)
                last.then_inc(prod_used, 1)

            def turn_y(s):
                pe.wait_ge(normed["y"], BLK * (s + 1))
                for i in range(2):
                    if i == 1:
                        after(pe, h2T_ready, s)
                    for j in range(2):
                        c = 2 * i + j
                        for k in range(BLK):
                            last = nc.tensor.transpose(AB[:, i, j * T + k * TB:j * T + (k + 1) * TB],
                                                       ysb[:, k, c * P:(c + 1) * P], idn[:TB, :TB])
                    last.then_inc(ynT_filled, 1)

            def project_out(s, q):
                pe.wait_ge(y3_ready, s + 1)
                for k in range(BLK):
                    tok = slice(k * TB, (k + 1) * TB)
                    for c in range(IC):
                        mm(AB[0:TB, 0, k * D:(k + 1) * D], lhsT=y3[:, c, tok], rhs=wout[:, c, :],
                           start=(k == 0 and c == 0), stop=False, skip_group_check=True)
                    for m in range(DC):
                        last = mm(AB[0:TB, 0, k * D + m * P:k * D + (m + 1) * P], lhsT=hT[q][:, m, tok], rhs=idn[:],
                                  start=False, stop=(m == DC - 1), skip_group_check=True)
                last.then_inc(out_filled, 1)

            def turn(o, src, done):
                for m in range(DC):
                    for k in range(BLK):
                        last = nc.tensor.transpose(o[:, m * T + k * TB:m * T + (k + 1) * TB],
                                                   src[:, k, m * P:(m + 1) * P], idn[:TB, :TB])
                last.then_inc(done, 1)

            def token_major(o, lhs, rhs, done):
                for k in range(BLK):
                    for c in range(DC):
                        last = mm(o[0:TB, k * D:(k + 1) * D], lhsT=lhs[:, c, k * TB:(k + 1) * TB], rhs=rhs[:, c, :],
                                  start=(c == 0), stop=(c == DC - 1))
                last.then_inc(done, 1)

            def scores(s, n):
                k, h0 = n // 2, HU * (n % 2)
                if n == 0:
                    pe.wait_ge(qm_ready, s + 1)
                    pe.wait_ge(vv_ready, s + 1)
                else:
                    pe.wait_ge(pT_ready, UNITS * s + n)
                for j in range(HU):
                    last = mm(BB[0:TB, j // 2, (j % 2) * T:(j % 2 + 1) * T],
                              lhsT=qm[:, h0 + j, k * TB:(k + 1) * TB], rhs=ks[:], start=True, stop=True)
                last.then_inc(s_filled, 1)

            def turn_probs(s, n):
                pe.wait_ge(pr_ready, UNITS * s + n + 1)
                for j in range(HU):
                    for k in range(BLK):
                        at = ((j % 2) * 2 + k) * TB
                        last = nc.tensor.transpose(BB[0:TB, j // 2, at:at + TB], pr[:, j, k * TB:(k + 1) * TB],
                                                   idn[:TB, :TB])
                last.then_inc(pT_filled, 1)

            def mix_values(s, n):
                h0 = HU * (n % 2)
                pe.wait_ge(pT_ready, UNITS * s + n + 1)
                if n == 0:
                    after(pe, moe_step, 17 * s)
                else:
                    pe.wait_ge(av_step, 3 * (UNITS * s + n))
                for j in range(HU):
                    for k in range(BLK):
                        at = ((j % 2) * 2 + k) * TB
                        last = mm(BB[0:TB, 2, j * DV:(j + 1) * DV], lhsT=pT[:, j // 2, at:at + TB],
                                  rhs=vs[:, k, (h0 + j) * DV:(h0 + j + 1) * DV], start=(k == 0), stop=(k == BLK - 1))
                last.then_inc(av_filled, 1)

            def gate(s):
                pe.wait_ge(h3T_ready, s + 1)
                for k in range(BLK):
                    for c in range(DC):
                        last = mm(BB[0:TB, 1, k * EXPERTS:(k + 1) * EXPERTS], lhsT=h3T[:, c, k * TB:(k + 1) * TB],
                                  rhs=wg[:, c, :], start=(c == 0), stop=(c == DC - 1))
                last.then_inc(gate_filled, 1)

            def expert_pair(s, m):
                pair, k = m // 2, m % 2
                if m == 1:
                    pe.wait_ge(h3T_ready, s + 1)
                if m == 4:
                    pe.wait_ge(wsT_ready, s + 1)
                prev = {2: 0, 3: 1, 5: 2, 6: 3, 7: 4}.get(m)
                if prev is not None:
                    pe.wait_ge(moe_step, 17 * s + 2 * prev + 2)
                for c in range(DC):
                    last = mm(BB[0:TB, MOE_BANK[m], :], lhsT=h3T[:, c, k * TB:(k + 1) * TB],
                              rhs=we[:, c, pair * 2 * D:(pair + 1) * 2 * D], start=(c == 0), stop=(c == DC - 1))
                last.then_inc(moe_filled, 1)

            def turn_gates(s):
                pe.wait_ge(gate_step, GSTEPS * (s + 1))
                for k in range(BLK):
                    last = nc.tensor.transpose(BB[0:EXPERTS, 1, k * TB:(k + 1) * TB], gw[:, k, :], idn[:TB, :TB])
                last.then_inc(wsT_filled, 1)

            def expert_biases(s):
                pe.wait_ge(moe_step, 17 * s + 2 * 5 + 2)
                for k in range(BLK):
                    last = mm(BB[0:TB, 2, k * D:(k + 1) * D], lhsT=wsT[:, k * TB:(k + 1) * TB], rhs=be[:],
                              start=True, stop=True)
                last.then_inc(moe_filled, 1)

            def prologue():
                pe.wait_ge(w_landed, W_ALL)
                pe.wait_ge(const_ready, CONSTS)
                patches(0, 0)
                patches(0, 1)
                embed(0)
                project_in(0, 0, U_XB, 0)
                project_in(0, 0, U_Z, IC)
                xproj(0)
                dt_row(0)
                for ng in range(GC - 1):
                    spread_bc(0, ng)

            def step(b, par, front, scan, a, b_head, b_rest):
                prev = not (isinstance(b, int) and (b == 0 or b > IMAGES))
                for g in range(GROUPS):
                    if scan and g == 0:
                        spread_bc(b, GC - 1)
                    if front and g in AT_BC:
                        spread_bc(b + 1, AT_BC[g])
                    if g == 0 and prev:
                        sum_states(b - 1, 1 - par, GROUPS - 1)
                    if g > 0 and scan:
                        sum_states(b, par, g - 1)
                    if front:
                        s, q = b + 1, 1 - par
                        if g in AT_PATCH:
                            patches(s, AT_PATCH[g])
                        if g == AT_EMBED:
                            embed(s)
                        if g == AT_XB:
                            project_in(s, q, U_XB, 0)
                        if g == AT_Z:
                            project_in(s, q, U_Z, IC)
                        if g == AT_XPROJ:
                            xproj(s)
                        if g == AT_DT:
                            dt_row(s)
                    if a:
                        s, q = b - 1, 1 - par
                        if g == AT_YNORM:
                            turn_y(s)
                        if g == AT_OUT:
                            project_out(s, q)
                        if g == AT_H1T:
                            pe.wait_ge(normed["out"], BLK * (s + 1))
                            turn(AB[:, 1, :], h1, h1T_filled)
                        if g == AT_RK:
                            pe.wait_ge(mix_step, 8 * (s + 1))
                            token_major(AB[:, 0, :], xr, wr, r_filled)
                            for m in range(DC):
                                for k in range(DC):
                                    last = mm(AB[:, 1, m * T:(m + 1) * T], lhsT=wk[:, k, m * P:(m + 1) * P],
                                              rhs=xk[:, k, :], start=(k == 0), stop=(k == DC - 1))
                            last.then_inc(k_filled, 1)
                        if g == AT_VMM:
                            pe.wait_ge(ksq_ready, s + 1)
                            pe.wait_ge(r_ready, s + 1)
                            token_major(AB[:, 0, :], ka, wv, v_filled)
                        if g == AT_H2T:
                            pe.wait_ge(normed["ffn"], BLK * (s + 1))
                            turn(AB[:, 1, :], h2, h2T_filled)
                    if b_rest:
                        s = b - 2
                        if g in AT_PT:
                            turn_probs(s, AT_PT[g])
                        if g in AT_AVS:
                            mix_values(s, AT_AVS[g])
                            scores(s, AT_AVS[g] + 1)
                        if g == AT_AV3:
                            mix_values(s, UNITS - 1)
                        if g == AT_H3T:
                            pe.wait_ge(normed["att"], BLK * (s + 1))
                            turn(BB[:, 0, :], h3, h3T_filled)
                        if g == AT_GATE:
                            gate(s)
                        if g == AT_WS:
                            turn_gates(s)
                        for m in AT_MOE.get(g, ()):
                            expert_pair(s, m)
                        if g == AT_BE:
                            expert_biases(s)
                    if b_head:
                        s = b - 1
                        if g == AT_QKV:
                            pe.wait_ge(h2T_ready, s + 1)
                            after(pe, moe_step, 17 * (s - 1) + 16)
                            for o, w in ((0, wq), (1, wkk)):
                                for k in range(DC):
                                    last = mm(BB[0:QK, 0, o * T:(o + 1) * T], lhsT=w[:, k, :], rhs=h2T[:, k, :],
                                              start=(k == 0), stop=(k == DC - 1))
                            last.then_inc(qk_filled, 1)
                            token_major(BB[:, 1, :], h2T, wvv, vv_filled)
                        if g == AT_S0:
                            scores(s, 0)
                        if g == AT_P0:
                            turn_probs(s, 0)
                        if g == AT_UNIT1:
                            mix_values(s, 0)
                            scores(s, 1)

            body.prologue, body.step = prologue, step
            schedule(body)

        @block.scalar
        def _(act):
            body = Body()
            body.eng = act
            go = nc.scalar.activation

            def filled(s, f):
                act.wait_ge(f_filled, USES * s + f + 1)
                return FB[:, f % 2, :]

            def drain_patches(s, h):
                for f in (2 * h, 2 * h + 1):
                    q0, q1 = PATCH_USES[f]
                    o = filled(s, U_PATCH + f)
                    go(patT[:, q0:q1, :], o[:, 0:(q1 - q0) * CROWS].rearrange("p (q r) -> p q r", r=CROWS),
                       ACT.Copy).then_inc(f_drained, 1)

            def drain_embed(s, q):
                after(act, out_filled, s - 1)
                for m in range(DC):
                    o = filled(s, U_EMBED + m)
                    go(hT[q][:, m, :], o[:, 0:T], ACT.Identity, bias=btok[:, m:m + 1]).then_inc(f_drained, 1)

            def drain_xb(s):
                after(act, conv_step, TAPS * IC * s)
                for f in range(2):
                    o = filled(s, U_XB + f)
                    go(xpad[:, 2 * f:2 * f + 2, TAPS - 1:], o[:, 0:2 * T].rearrange("p (c t) -> p c t", c=2),
                       ACT.Copy).then_inc(f_drained, 1)

            def drain_z(s, q):
                after(act, y3_ready, s - 1)
                for f in range(2):
                    o = filled(s, U_Z + f)
                    go(zs[q][:, 2 * f:2 * f + 2, :], o[:, 0:2 * T].rearrange("p (c t) -> p c t", c=2),
                       ACT.Silu).then_inc(f_drained, 1)

            def silu_x(s):
                act.wait_ge(conv_step, TAPS * IC * (s + 1))
                go(xbs[:], xbs[:], ACT.Silu).then_inc(silu_ready, 1)

            def drain_proj(s):
                o = filled(s, U_XPROJ)
                after(act, split_step, 4 * s)
                go(pj[:], o[0:STK, 0:T], ACT.Copy).then_inc(f_drained, 1)

            def times_d(s, q):
                act.wait_ge(silu_ready, s + 1)
                after(act, prod_used, GROUPS * (s - 1))
                for c in range(IC):
                    last = go(xD[q][:, c, :], xbs[:, c, :], ACT.Copy, scale=dpar[:, c:c + 1])
                last.then_inc(xD_ready, 1)

            def drain_dt(s):
                o = filled(s, U_DT)
                after(act, dt_ready, s)
                go(dtin[:], o[:, 0:T], ACT.Copy).then_inc(f_drained, 1)

            def softplus(s):
                act.wait_ge(f_drained, USES * s + U_BC)
                for c in range(IC):
                    last = go(soft[:, c, :], dtin[:], ACT.Abs, scale=dtw[:, c:c + 1], bias=dtb[:, c:c + 1])
                last.then_inc(soft_step, 1)
                act.wait_ge(soft_step, 3 * s + 1)
                go(soft[:], soft[:], ACT.Exp, scale=-1.0).then_inc(soft_step, 1)
                act.wait_ge(soft_step, 3 * s + 2)
                go(soft[:], soft[:], ACT.Ln, bias=1.0).then_inc(soft_step, 1)

            def drain_bc(s, ng):
                for i in range(4):
                    f = U_BC + 4 * ng + i
                    o = filled(s, f)
                    n0 = NG * ng + 2 * (i % 2)
                    if i == 0:
                        after(act, xs_ready, GROUPS * s - GC + ng + 1)
                    if i == 2:
                        after(act, prod_ready, GROUPS * s - GC + ng + 1)
                    go((Bb, Cb)[i // 2][:, n0:n0 + 2, :], o[:, 0:2 * T].rearrange("p (c t) -> p c t", c=2),
                       ACT.Copy).then_inc(f_drained, 1)

            def decay(s, q, g):
                c = g // GC
                if g == 0:
                    act.wait_ge(dt_ready, s + 1)
                after(act, scan_done, GROUPS * s + g + 1 - DRING)
                for j in range(NG):
                    n = NG * (g % GC) + j
                    last = go(dA[g % DRING][:, j, 1:T], dt_[q][:, c, 1:T], ACT.Exp, scale=negA[:, c, n:n + 1])
                last.then_inc(dA_ready, 1)

            def drain_y(s, c):
                act.wait_ge(prod_used, GROUPS * s + GC * (c + 1))
                if c == 0:
                    after(act, ynT_filled, 2 * s)
                go(ysb[:, :, c * P:(c + 1) * P], YB[0:TB, 0:BLK * P].rearrange("p (k d) -> p k d", k=BLK),
                   ACT.Copy).then_inc(y_drained, 1)

            def inverse_std(s, n):
                act.wait_ge(stats_step[n], 4 * (s + 1))
                go(lnv[n][:], mv[n][:, :, 1], ACT.Ln, bias=epsc[0:TB, :]).then_inc(rstd_step[n], 1)
                act.wait_ge(rstd_step[n], 2 * s + 1)
                go(rstd[n][:], lnv[n][:], ACT.Exp, scale=-0.5).then_inc(rstd_step[n], 1)

            def drain_turned(o, dst, filled_sem, ready, s):
                act.wait_ge(filled_sem, s + 1)
                go(dst, o[:, 0:DC * T].rearrange("p (c t) -> p c t", c=DC), ACT.Copy).then_inc(ready, 1)

            def slope(s, n):
                act.wait_ge(s_filled, UNITS * s + n + 1)
                go(pr[:].rearrange("p (a b) t -> p a (b t)", a=2), BB[0:TB, 0:2, 0:2 * T], ACT.Copy,
                   scale=SLOPE).then_inc(slope_ready, 1)

            def probs(s, n):
                act.wait_ge(nmx_ready, UNITS * s + n + 1)
                for j in range(HU):
                    last = go(pr[:, j, :], pr[:, j, :], ACT.Exp, bias=nmx[:, j:j + 1], accum_out=sums[:, j:j + 1])
                last.then_inc(pr_ready, 1)

            def drain_pT(s, n):
                act.wait_ge(pT_filled, UNITS * s + n + 1)
                go(pT[:], BB[0:TB, 0:2, 0:2 * T], ACT.Copy).then_inc(pT_ready, 1)

            def prologue():
                act.wait_ge(w_landed, W_ALL)
                go(negA[:], negA[:], ACT.Exp).then_inc(nega_exp, 1)
                act.wait_ge(zeros_ready, 1)
                act.wait_ge(const_ready, CONSTS)
                drain_patches(0, 0)
                drain_patches(0, 1)
                drain_embed(0, 0)
                drain_xb(0)
                drain_z(0, 0)
                silu_x(0)
                drain_proj(0)
                times_d(0, 0)
                drain_dt(0)
                softplus(0)
                for ng in range(GC - 1):
                    drain_bc(0, ng)
                decay(0, 0, 0)

            def step(b, par, front, scan, a, b_head, b_rest):
                prev = not (isinstance(b, int) and (b == 0 or b > IMAGES))
                for g in range(GROUPS):
                    if scan and g == 0:
                        drain_bc(b, GC - 1)
                    if front and g in AT_BC:
                        drain_bc(b + 1, AT_BC[g])
                    if scan and g < GROUPS - 1:
                        decay(b, par, g + 1)
                    elif front and g == GROUPS - 1:
                        decay(b + 1, 1 - par, 0)
                    if g == 0 and prev:
                        drain_y(b - 1, IC - 1)
                    if scan and g > 0 and g % GC == 0:
                        drain_y(b, g // GC - 1)
                    if front:
                        s, q = b + 1, 1 - par
                        if g in AT_PATCH:
                            drain_patches(s, AT_PATCH[g])
                        if g == AT_EMBED:
                            drain_embed(s, q)
                        if g == AT_XB:
                            drain_xb(s)
                        if g == AT_SILU:
                            drain_z(s, q)
                            silu_x(s)
                        if g == AT_XPROJ:
                            drain_proj(s)
                            times_d(s, q)
                        if g == AT_DT:
                            drain_dt(s)
                        if g == AT_SOFT:
                            softplus(s)
                    if a:
                        s = b - 1
                        if g == AT_YSTATS:
                            inverse_std(s, "y")
                        if g == AT_YNORM:
                            for i in range(2):
                                act.wait_ge(ynT_filled, 2 * s + i + 1)
                                for j in range(2):
                                    c = 2 * i + j
                                    last = go(y3[:, c, :], AB[:, i, j * T:(j + 1) * T], ACT.Identity,
                                              scale=lng[:, c:c + 1], bias=lnb[:, c:c + 1])
                                last.then_inc(yg_ready, 1)
                        if g == AT_LN1:
                            inverse_std(s, "out")
                        if g == AT_H1T:
                            drain_turned(AB[:, 1, :], h1T[:, :, 1:], h1T_filled, h1T_ready, s)
                        if g == AT_RK:
                            act.wait_ge(r_filled, s + 1)
                            go(rs[:], AB[0:TB, 0, :].rearrange("p (k d) -> p k d", k=BLK),
                               ACT.Sigmoid).then_inc(r_ready, 1)
                            act.wait_ge(k_filled, s + 1)
                            go(ka[:], AB[:, 1, 0:DC * T].rearrange("p (c t) -> p c t", c=DC),
                               ACT.Relu).then_inc(krelu_ready, 1)
                        if g == AT_LN2:
                            inverse_std(s, "ffn")
                        if g == AT_H2T:
                            drain_turned(AB[:, 1, :], h2T[:], h2T_filled, h2T_ready, s)
                    if b_rest:
                        s = b - 2
                        if g in AT_PT:
                            drain_pT(s, AT_PT[g])
                        if g in AT_AVS:
                            slope(s, AT_AVS[g] + 1)
                            probs(s, AT_AVS[g] + 1)
                        if g == AT_AV3:
                            inverse_std(s, "att")
                        if g == AT_H3T:
                            drain_turned(BB[:, 0, :], h3T[:], h3T_filled, h3T_ready, s)
                        if g == AT_GATE:
                            act.wait_ge(gate_step, GSTEPS * s + 3)
                            go(gl[:], gl[:], ACT.Exp).then_inc(gate_exp, 1)
                        if g == AT_WS:
                            act.wait_ge(wsT_filled, s + 1)
                            go(wsT[:], BB[0:EXPERTS, 1, 0:T], ACT.Copy).then_inc(wsT_ready, 1)
                        if g == AT_BE:
                            inverse_std(s, "moe")
                    if b_head:
                        s = b - 1
                        if g == AT_QKV:
                            act.wait_ge(qk_filled, s + 1)
                            go(qs[:], BB[0:QK, 0, 0:T], ACT.Identity, bias=bq[:])
                            go(ks[:], BB[0:QK, 0, T:2 * T], ACT.Identity, bias=bk[:]).then_inc(qk_ready, 1)
                        if g == AT_S0:
                            slope(s, 0)
                            probs(s, 0)
                        if g == AT_P0:
                            drain_pT(s, 0)
                        if g == AT_UNIT1:
                            slope(s, 1)
                            probs(s, 1)

            body.prologue, body.step = prologue, step
            schedule(body)

        @block.vector
        def _(dve):
            body = Body()
            body.eng = dve
            v = nc.vector

            def taps(s):
                after(dve, u_ready, s)
                after(dve, xD_ready, s)
                after(dve, f_filled, USES * (s - 1) + U_XPROJ + 1 if not (isinstance(s, int) and s == 0) else 0)
                for k in range(TAPS):
                    for c in range(IC):
                        if k == 0:
                            dve.wait_ge(f_drained, USES * s + U_XB + c // 2 + 1)
                            v.tensor_scalar(xbs[:, c, :], xpad[:, c, 0:T], cw[:, c, 0:1], cb[:, c:c + 1],
                                            ALU.mult, ALU.add).then_inc(conv_step, 1)
                        else:
                            dve.wait_ge(conv_step, TAPS * IC * s + IC * (k - 1) + c + 1)
                            v.scalar_tensor_tensor(out=xbs[:, c, :], in0=xpad[:, c, k:k + T],
                                                   scalar=cw[:, c, k:k + 1], in1=xbs[:, c, :], op0=ALU.mult,
                                                   op1=ALU.add).then_inc(conv_step, 1)

            def split(s):
                dve.wait_ge(f_drained, USES * s + U_XPROJ + 1)
                after(dve, f_filled, USES * s)
                v.tensor_copy(hi1[:], pj[:]).then_inc(split_step, 1)
                dve.wait_ge(split_step, 4 * s + 1)
                v.scalar_tensor_tensor(out=pj1[:], in0=hi1[:], scalar=spl[:, 0:1], in1=pj[:], op0=ALU.mult,
                                       op1=ALU.add).then_inc(split_step, 1)
                dve.wait_ge(split_step, 4 * s + 2)
                v.tensor_copy(hi2[:], pj1[:]).then_inc(split_step, 1)
                dve.wait_ge(split_step, 4 * s + 3)
                v.scalar_tensor_tensor(out=stack[:], in0=hi2[:], scalar=spl[:, 1:2], in1=pj1[:], op0=ALU.mult,
                                       op1=ALU.add).then_inc(split_step, 1)

            def step_size(s, q):
                dve.wait_ge(f_drained, USES * s + U_BC)
                after(dve, dA_ready, GROUPS * (s - 1))
                after(dve, u_ready, s - 1)
                for c in range(IC):
                    last = v.tensor_scalar(dt_[q][:, c, :], dtin[:], dtw[:, c:c + 1], dtb[:, c:c + 1],
                                           ALU.mult, ALU.add)
                last.then_inc(lin_ready, 1)
                dve.wait_ge(lin_ready, s + 1)
                dve.wait_ge(soft_step, 3 * (s + 1))
                v.scalar_tensor_tensor(out=dt_[q][:], in0=dt_[q][:], scalar=0.0, in1=soft[:], op0=ALU.max,
                                       op1=ALU.add).then_inc(dt_ready, 1)

            def inputs(s, q, g):
                c, ng = g // GC, g % GC
                if g == 0:
                    dve.wait_ge(u_ready, s + 1)
                if c == 0:
                    dve.wait_ge(f_drained, USES * s + U_BC + 4 * ng + 2)
                after(dve, prod_used, GROUPS * s + g + 1 - RING)
                v.tensor_tensor(X[g % RING][:], u[q][:, c:c + 1, :].broadcast_to([P, NG, T]),
                                Bb[:, NG * ng:NG * (ng + 1), :], ALU.mult).then_inc(xs_ready, 1)

            def scan_group(s, g):
                dve.wait_ge(xs_ready, GROUPS * s + g + 1)
                dve.wait_ge(dA_ready, GROUPS * s + g + 1)
                t = X[g % RING][:].rearrange("p n t -> p (n t)")
                v.tensor_tensor_scan(t, dA[g % DRING][:].rearrange("p n t -> p (n t)"), t, 0.0, ALU.mult,
                                     ALU.add).then_inc(scan_done, 1)

            def moments(s, n, src):
                for k in range(BLK):
                    v.bn_stats(stat[n][:, k, :], src(k)).then_inc(stats_step[n], 1)
                dve.wait_ge(stats_step[n], 4 * s + BLK)
                dve.sem_inc(dve_past, 1)
                for k in range(BLK):
                    v.bn_aggr(mv[n][:, k, :], stat[n][:, k, :]).then_inc(stats_step[n], 1)

            def normalise(s, n, src, dst):
                dve.wait_ge(rstd_step[n], 2 * (s + 1))
                for k in range(BLK):
                    v.tensor_scalar(dst[:, k, :], src(k), mv[n][:, k, 0:1], rstd[n][:, k:k + 1], ALU.subtract,
                                    ALU.mult).then_inc(normed[n], 1)

            def token_mix(s):
                dve.wait_ge(h1T_ready, s + 1)
                for i, (dst, om) in enumerate(((xr, omr), (xk, omk))):
                    for m in range(DC):
                        v.tensor_scalar(dst[:, m, :], h1T[:, m, 0:T], om[:, m:m + 1], None,
                                        ALU.mult).then_inc(mix_step, 1)
                for i, (dst, mu) in enumerate(((xr, mur), (xk, muk))):
                    for m in range(DC):
                        dve.wait_ge(mix_step, 8 * s + 2 * i + m + 1)
                        v.scalar_tensor_tensor(out=dst[:, m, :], in0=h1T[:, m, 1:], scalar=mu[:, m:m + 1],
                                               in1=dst[:, m, :], op0=ALU.mult, op1=ALU.add).then_inc(mix_step, 1)

            def ffn_sum(s):
                dve.wait_ge(v_filled, s + 1)
                dve.wait_ge(r_ready, s + 1)
                v.tensor_tensor(rs[:], AB[0:TB, 0, :].rearrange("p (k d) -> p k d", k=BLK), rs[:],
                                ALU.mult).then_inc(ffn_step, 1)
                dve.wait_ge(ffn_step, 2 * s + 1)
                v.tensor_tensor(rs[:], rs[:], h1[:], ALU.add).then_inc(ffn_step, 1)
                dve.wait_ge(ffn_step, 2 * s + 2)

            def heads(s):
                dve.wait_ge(qk_ready, s + 1)
                for h in range(HEADS):
                    last = v.tensor_scalar(qm[:, h, :], qs[:], hm[:, h:h + 1], None, ALU.mult)
                last.then_inc(qm_ready, 1)
                dve.wait_ge(vv_filled, s + 1)
                v.tensor_tensor(vs[:], BB[0:TB, 1, :].rearrange("p (k d) -> p k d", k=BLK),
                                bv[:, None, :].broadcast_to([TB, BLK, D]), ALU.add).then_inc(vv_ready, 1)

            def leaky(s, n):
                dve.wait_ge(slope_ready, UNITS * s + n + 1)
                pv = pr[:].rearrange("p (a b) t -> p a (b t)", a=2)
                v.tensor_tensor(pv, BB[0:TB, 0:2, 0:2 * T], pv, ALU.max).then_inc(leaky_ready, 1)
                dve.wait_ge(leaky_ready, UNITS * s + n + 1)
                v.tensor_reduce(nmx[:], pr[:], AX_X, ALU.max, negate=True).then_inc(nmx_ready, 1)

            def attended(s, n):
                k, h0 = n // 2, HU * (n % 2)
                base = 3 * (UNITS * s + n)
                dve.wait_ge(pr_ready, UNITS * s + n + 1)
                v.reciprocal(rg[:], sums[:]).then_inc(av_step, 1)
                dve.wait_ge(av_step, base + 1)
                v.tensor_scalar(rg[:], rg[:], gam[:], None, ALU.mult).then_inc(av_step, 1)
                dve.wait_ge(av_step, base + 2)
                dve.wait_ge(av_filled, UNITS * s + n + 1)
                v.tensor_tensor(att[:, k, h0 * DV:(h0 + HU) * DV].rearrange("p (h d) -> p h d", h=HU),
                                BB[0:TB, 2, 0:HU * DV].rearrange("p (h d) -> p h d", h=HU),
                                rg[:].rearrange("p (h o) -> p h o", o=1).broadcast_to([TB, HU, DV]),
                                ALU.mult).then_inc(av_step, 1)

            def gates(s):
                n = [GSTEPS * s]

                def then(ins):
                    ins.then_inc(gate_step, 1)
                    n[0] = n[0] + 1
                    dve.wait_ge(gate_step, n[0])

                def wide(i):
                    return gs[:, i, :].rearrange("p (k o) -> p k o", o=1).broadcast_to([TB, BLK, EXPERTS])

                dve.wait_ge(gate_filled, s + 1)
                then(v.tensor_tensor(gl[:], BB[0:TB, 1, 0:BLK * EXPERTS].rearrange("p (k e) -> p k e", k=BLK),
                                     bg[:], ALU.add))
                then(v.tensor_reduce(gs[:, 0, :], gl[:], AX_X, ALU.max))
                then(v.tensor_tensor(gl[:], gl[:], wide(0), ALU.subtract))
                dve.wait_ge(gate_exp, s + 1)
                then(v.tensor_reduce(gs[:, 1, :], gl[:], AX_X, ALU.add))
                then(v.reciprocal(gs[:, 1, :], gs[:, 1, :]))
                then(v.tensor_tensor(gl[:], gl[:], wide(1), ALU.mult))
                then(v.tensor_reduce(gs[:, 2, :], gl[:], AX_X, ALU.max))
                for i, (src, oh) in enumerate(((gl, oh1), (g2, oh2))):
                    then(v.tensor_tensor(oh[:], src[:], wide(2 + 2 * i), ALU.is_equal))
                    then(v.tensor_tensor(oh[:], oh[:], rk[:], ALU.mult))
                    then(v.tensor_reduce(gs[:, 3, :], oh[:], AX_X, ALU.max))
                    then(v.tensor_tensor(oh[:], rk[:], wide(3), ALU.is_equal))
                    if i == 0:
                        then(v.scalar_tensor_tensor(out=g2[:], in0=oh[:], scalar=-2.0, in1=gl[:], op0=ALU.mult,
                                                    op1=ALU.add))
                        then(v.tensor_reduce(gs[:, 4, :], g2[:], AX_X, ALU.max))
                v.tensor_tensor(oh1[:], oh1[:], oh2[:], ALU.add)
                then(v.tensor_tensor(gs[:, 5, :], gs[:, 2, :], gs[:, 4, :], ALU.add))
                v.tensor_tensor(gw[:], oh1[:], gl[:], ALU.mult)
                then(v.reciprocal(gs[:, 5, :], gs[:, 5, :]))
                v.tensor_tensor(gw[:], gw[:], wide(5), ALU.mult).then_inc(gate_step, 1)

            def add_pair(s, m):
                pair, k = m // 2, m % 2
                bank = MOE_BANK[m]
                if m == 0:
                    dve.wait_ge(gate_step, GSTEPS * (s + 1))
                dve.wait_ge(moe_filled, 9 * s + m + 1)
                for e in range(2):
                    if m >= 2 or e == 1:
                        dve.wait_ge(moe_step, 17 * s + 2 * m + e if e else 17 * s + 2 * (m - 2) + 2)
                    src = h3 if m < 2 and e == 0 else acc
                    v.scalar_tensor_tensor(out=acc[:, k, :], in0=BB[0:TB, bank, e * D:(e + 1) * D],
                                           scalar=gw[:, k, 2 * pair + e:2 * pair + e + 1], in1=src[:, k, :],
                                           op0=ALU.mult, op1=ALU.add).then_inc(moe_step, 1)

            def add_biases(s):
                dve.wait_ge(moe_filled, 9 * (s + 1))
                dve.wait_ge(moe_step, 17 * s + 16)
                v.tensor_tensor(acc[:], BB[0:TB, 2, :].rearrange("p (k d) -> p k d", k=BLK), acc[:],
                                ALU.add).then_inc(moe_step, 1)
                dve.wait_ge(moe_step, 17 * (s + 1))

            def prologue():
                dve.wait_ge(w_landed, W_ALL)
                dve.wait_ge(nega_exp, 1)
                v.tensor_scalar(negA[:], negA[:], -1.0, None, ALU.mult).then_inc(const_ready, 1)
                v.tensor_scalar(omr[:], mur[:], -1.0, 1.0, ALU.mult, ALU.add).then_inc(const_ready, 1)
                v.tensor_scalar(omk[:], muk[:], -1.0, 1.0, ALU.mult, ALU.add).then_inc(const_ready, 1)
                v.tensor_scalar(hm[:], hm[:], 1.0, None, ALU.mult).then_inc(const_ready, 1)
                v.tensor_copy(sel[:], selF[:]).then_inc(const_ready, 1)
                dve.wait_ge(const_ready, CONSTS)
                dve.wait_ge(zeros_ready, 1)
                taps(0)
                split(0)
                step_size(0, 0)
                inputs(0, 0, 0)

            def step(b, par, front, scan, a, b_head, b_rest):
                for g in range(GROUPS):
                    if scan and g < GROUPS - 1:
                        inputs(b, par, g + 1)
                    elif front and g == GROUPS - 1:
                        inputs(b + 1, 1 - par, 0)
                    if scan:
                        scan_group(b, g)
                    if front:
                        s, q = b + 1, 1 - par
                        if g == AT_CONV:
                            taps(s)
                        if g == AT_SPLIT:
                            split(s)
                        if g == AT_SOFT:
                            step_size(s, q)
                    if a:
                        s = b - 1
                        if g == AT_YSTATS:
                            dve.wait_ge(y_drained, IC * (s + 1))
                            moments(s, "y", lambda k: ysb[:, k, :])
                        if g == AT_YNORM:
                            normalise(s, "y", lambda k: ysb[:, k, :], ysb)
                        if g == AT_LN1:
                            dve.wait_ge(out_filled, s + 1)
                            moments(s, "out", lambda k: AB[0:TB, 0, k * D:(k + 1) * D])
                            normalise(s, "out", lambda k: AB[0:TB, 0, k * D:(k + 1) * D], h1)
                        if g == AT_H1T:
                            token_mix(s)
                        if g == AT_VMM:
                            ffn_sum(s)
                            moments(s, "ffn", lambda k: rs[:, k, :])
                        if g == AT_LN2:
                            normalise(s, "ffn", lambda k: rs[:, k, :], h2)
                    if b_rest:
                        s = b - 2
                        if g in AT_AVS:
                            attended(s, AT_AVS[g])
                            leaky(s, AT_AVS[g] + 1)
                        if g == AT_AV3:
                            attended(s, UNITS - 1)
                            dve.wait_ge(av_step, 3 * UNITS * (s + 1))
                            v.scalar_tensor_tensor(out=att[:], in0=h2_of_b[:], scalar=2.0, in1=att[:], op0=ALU.mult,
                                                   op1=ALU.add).then_inc(att_sum, 1)
                            dve.wait_ge(att_sum, s + 1)
                            moments(s, "att", lambda k: att[:, k, :])
                            normalise(s, "att", lambda k: att[:, k, :], h3)
                        if g == AT_GATE:
                            gates(s)
                        for m in AT_ADD.get(g, ()):
                            add_pair(s, m)
                        if g == AT_BE:
                            add_biases(s)
                            moments(s, "moe", lambda k: acc[:, k, :])
                        if g == AT_BE + 1:
                            after(dve, out_landed, 16 * s)
                            normalise(s, "moe", lambda k: acc[:, k, :], ob)
                    if b_head:
                        s = b - 1
                        if g == AT_QKV:
                            heads(s)
                        if g == AT_S0:
                            leaky(s, 0)
                        if g == AT_UNIT1:
                            attended(s, 0)
                            leaky(s, 1)

            h2_of_b = h2
            body.prologue, body.step = prologue, step
            schedule(body)


_INS = ["x", "w_tok", "b_tok", "w_in", "conv_w", "conv_b", "w_xproj", "a_log", "d_par", "dt_w", "dt_b", "w_out",
        "ln_g", "ln_b", "w_r", "w_k", "w_v", "mu_r", "mu_k", "w_q", "b_q", "w_kk", "b_k", "w_vv", "b_v", "gamma",
        "w_g", "b_g", "w_e", "b_e", "ident", "select", "split_masks", "head_mask", "rank"]


def kernel(**inputs):
    import numpy as np
    import concourse.bacc as _bacc
    from concourse import mybir as _mybir
    from concourse.bass_utils import run_bass_kernel_spmd as _run

    a = {k: np.asarray(v) for k, v in inputs.items()}

    def cols(w):
        return w.reshape(w.shape[0] // P, P, *w.shape[1:]).swapaxes(0, 1)

    f = np.float32
    rows = np.arange(STK)
    laid = {
        "x": a["x"].reshape(IMAGES * CROWS, PATCH * WIDTH),
        "w_tok": cols(a["L0_tok_W"].T),
        "b_tok": cols(a["L0_tok_b"]),
        "w_in": cols(a["L0_attn_in_proj_w"].T),
        "conv_w": cols(a["L0_attn_conv_w"]),
        "conv_b": cols(a["L0_attn_conv_b"]),
        "w_xproj": cols(np.tile(a["L0_attn_x_proj_w"].T, (1, PARTS))),
        "a_log": cols(a["L0_attn_A_log"]),
        "d_par": cols(a["L0_attn_D_param"]),
        "dt_w": cols(a["L0_attn_dt_w"][:, 0]),
        "dt_b": cols(a["L0_attn_dt_b"]),
        "w_out": cols(a["L0_attn_out_w"].T),
        "ln_g": cols(a["L0_attn_ln_g"]),
        "ln_b": cols(a["L0_attn_ln_b"]),
        "w_r": cols(a["L0_ffn_W_r"].T),
        "w_k": cols(a["L0_ffn_W_k"].T),
        "w_v": cols(a["L0_ffn_W_v"].T),
        "mu_r": cols(a["L0_ffn_mu_r"]),
        "mu_k": cols(a["L0_ffn_mu_k"]),
        "w_q": cols(a["L1_attn_Wq"].T),
        "b_q": a["L1_attn_bq"].reshape(QK, 1),
        "w_kk": cols(a["L1_attn_Wk"].T),
        "b_k": a["L1_attn_bk"].reshape(QK, 1),
        "w_vv": cols(a["L1_attn_Wv"].T),
        "b_v": np.tile(a["L1_attn_bv"], (TB, 1)),
        "gamma": np.tile(a["L1_attn_gamma"], (TB, 1)),
        "w_g": cols(a["L1_ffn_Wg"]),
        "b_g": np.tile(a["L1_ffn_bg"], (TB, BLK, 1)),
        "w_e": cols(a["L1_ffn_We"].transpose(2, 0, 1).reshape(D, EXPERTS * D)),
        "b_e": a["L1_ffn_be"],
        "ident": np.eye(P, dtype=f),
        "select": (rows[:, None] % PROJ == np.arange(PROJ)[None, :]).astype(f),
        "split_masks": -np.stack([rows >= PROJ, rows >= 2 * PROJ], 1).astype(f),
        "head_mask": ((np.arange(QK)[:, None] // (QK // HEADS)) == np.arange(HEADS)[None, :]).astype(f)
        * f((QK // HEADS) ** -0.5),
        "rank": np.tile(np.arange(EXPERTS, 0, -1, dtype=f), (TB, BLK, 1)),
    }
    nc = _bacc.Bacc("TRN2", target_bir_lowering=False, num_devices=1)
    arrays, args = {}, []
    for name in _INS:
        w = np.ascontiguousarray(laid[name])
        arrays[f"in_{name}"] = w
        args.append(nc.dram_tensor(f"in_{name}", w.shape, _mybir.dt.from_np(w.dtype), kind="ExternalInput").ap())
    out = nc.dram_tensor("out_0", (IMAGES * T, D), F32, kind="ExternalOutput").ap()
    vit_tower(nc, *args, out)
    r = _run(nc, [arrays], core_ids=[0])
    return r.results[0]["out_0"].reshape(IMAGES, T, D)
```

```python
from contextlib import ExitStack

import concourse.bass as bass
from concourse import mybir

F32 = mybir.dt.float32
BF16 = mybir.dt.bfloat16
ALU = mybir.AluOpType
ACT = mybir.ActivationFunctionType
AX_X = mybir.AxisListType.X

P = 128
IMAGES = 64
COLORS = 3
SIDE = 14
PATCH = 16
WIDTH = SIDE * PATCH
T = SIDE * SIDE
BLK = 2
TB = T // BLK
D = 256
DC = D // P
INNER = 512
IC = INNER // P
STATES = 16
TAPS = 4
HALVES = 2
ROWS = PATCH // HALVES
KP = COLORS * HALVES
CROWS = COLORS * SIDE
PROJ = 2 * STATES + 1
PARTS = 3
STK = PARTS * PROJ
NG = 4
GC = STATES // NG
GROUPS = IC * GC
RING = 4
DRING = 2
HEADS = 8
QK = D // HEADS
DV = D // HEADS
HU = 4
UNITS = BLK * (HEADS // HU)
EXPERTS = 8
PAIRS = EXPERTS // 2 * BLK
GSTEPS = 19
GIN = 2
LN_EPS = 1e-5
SLOPE = 0.2

POOL_INPUTS = (0, 1, 2, 3, 4, 5, 6, 11, 12, 13, 14, 15)
DVE_INPUTS = tuple(g for g in range(GROUPS) if g not in POOL_INPUTS)
FOLDED = (0, 6, 7, 8)

AT_REORDER = (-30, -27)
AT_PATCH, AT_PATCH_OUT = (-28, -26), (-27, -25)
AT_EMBED, AT_EMBED_OUT = -24, -23
AT_XB, AT_XB_OUT = -22, -20
AT_TAPS = {-18: (0, 1), -17: (2, 3)}
AT_TANH_X, AT_GATE_X, AT_XD = -16, -15, -10
AT_XPROJ, AT_XPROJ_OUT, AT_SPLIT = -14, -13, -12
AT_DT, AT_DT_OUT, AT_STEP, AT_U = -11, -10, -7, -4
AT_B = (-5, -4, -3, -1)
AT_C = (-2, 0, 1, 2)
AT_KEEP = 1
AT_Y_OUT = tuple(GC * (c + 1) + 2 for c in range(IC))
AT_Z, AT_Z_OUT = 19, 20
AT_Y_STATS, AT_Y_STD, AT_Y_NORM = 19, 20, 21
AT_TURN_Y, AT_YG, AT_Y3, AT_OUT = 22, 23, 24, 25
AT_OUT_STATS, AT_OUT_STD, AT_OUT_NORM = 26, 27, 28
AT_H1T, AT_H1T_OUT, AT_MIX = 29, 30, 31
AT_RK, AT_RK_OUT, AT_KSQ, AT_V = 32, 33, 35, 36
AT_FFN, AT_FFN_STATS, AT_FFN_STD, AT_FFN_NORM = 37, 38, 39, 40
AT_H2T, AT_H2T_OUT, AT_QK, AT_QK_OUT, AT_HEADS = 41, 42, 43, 44, 45
AT_VALUES, AT_VALUES_OUT = 44, 46
AT_SCORES = (46, 49, 53, 56)
AT_TURN_P = (51, 55, 60, 63)
AT_AV = (55, 57, 62, 65)
AT_ATT, AT_ATT_STD, AT_ATT_NORM = 67, 68, 70
AT_H3T, AT_H3T_OUT = 71, 73
AT_GATE, AT_GATE_IN, AT_GATE_EXP, AT_TOP2 = 74, 75, 76, 77
AT_WS, AT_WS_OUT = 79, 80
AT_PAIR = (77, 78, 79, 81, 83, 84, 85, 86)
AT_BE, AT_BE_OUT = 87, 88
AT_MOE_STATS, AT_MOE_STD, AT_MOE_NORM = 89, 90, 91
FIRST = AT_REORDER[0] // GROUPS
LAST = IMAGES - 1 + AT_MOE_NORM // GROUPS
LOOP_FROM = AT_MOE_NORM // GROUPS + 2
LOOP_PAIRS = (IMAGES + FIRST - 1 - LOOP_FROM) // 2

F0_USES = {"patch0": AT_PATCH[0], "patch1": AT_PATCH[1], "embed": AT_EMBED, "xb": AT_XB, "z": AT_Z, "be": AT_BE,
           **{f"B{i}": AT_B[i] for i in range(GC)}, **{f"C{i}": AT_C[i] for i in range(GC)}}
F1_USES = {**{n: at for n, at in F0_USES.items() if n != "be"}, "dt": AT_DT}
A0_USES = {"turn_y": AT_TURN_Y, "out": AT_OUT, "r": AT_RK, "v": AT_V, "values": AT_VALUES, "h3T": AT_H3T,
           "ws": AT_WS, "pair3": AT_PAIR[3], "pair6": AT_PAIR[6]}
A1_USES = {"turn_y": AT_TURN_Y, "h1T": AT_H1T, "k": AT_RK, "xproj": AT_XPROJ, "h2T": AT_H2T, "qk": AT_QK,
           "pair1": AT_PAIR[1], "pair4": AT_PAIR[4]}
M_USES = {"gate": AT_GATE, **{f"AV{n}": AT_AV[n] for n in range(UNITS)},
          **{f"pair{m}": AT_PAIR[m] for m in (0, 2, 5, 7)}}
S_USES = {**{f"S{n}": AT_SCORES[n] for n in range(UNITS)}, **{f"P{n}": AT_TURN_P[n] for n in range(UNITS)}}


def after(eng, sem, count):
    if isinstance(count, int) and count <= 0:
        return
    eng.wait_ge(sem, count)


def image_of(b, slot):
    off = slot // GROUPS
    return b - off if off > 0 else b + (-off) if off < 0 else b


def live(b, par, g, slot):
    if (slot - g) % GROUPS:
        return ()
    s = image_of(b, slot)
    if isinstance(s, int) and not 0 <= s < IMAGES:
        return ()
    return ((s, (par - slot // GROUPS) % 2),)


def rank(groups, g):
    return sum(x <= g for x in groups)


class Bank:

    def __init__(self, tile, uses, filled, drained):
        assert len({at % GROUPS for at in uses.values()}) == len(uses)
        self.tile, self.uses, self.filled, self.drained = tile, uses, filled, drained

    def count(self, name, s):
        at = self.uses[name]
        ahead = [at // GROUPS - other // GROUPS + (other % GROUPS <= at % GROUPS) for other in self.uses.values()]
        if isinstance(s, int):
            return sum(min(max(s + n, 0), IMAGES) for n in ahead)
        return s * len(ahead) + sum(ahead)


def vit_tower(nc, x, w_tok, b_tok, w_in, conv_w, conv_b, w_xproj, a_log, d_par, dt_w, dt_b, w_out, ln_g, ln_b,
              w_r, w_k, w_v, mu_r, mu_k, w_qk, b_q, b_k, w_vv, b_v, gamma, w_g, b_g, w_e, b_e,
              ident, select, split_masks, head_mask, rank_of, out):
    with ExitStack() as ctx:
        def sb(name, shape, dt=F32):
            return ctx.enter_context(nc.sbuf_tensor(name, shape, dt))

        def psum(name, shape):
            return ctx.enter_context(nc.psum_tensor(name, shape, F32))

        def sem(name):
            return ctx.enter_context(nc.semaphore(name))

        wtok = sb("wtok", [P, KP, D])
        btok = sb("btok", [P, DC])
        win = sb("win", [P, DC, 2 * INNER])
        cw = sb("cw", [P, IC, TAPS])
        cb = sb("cb", [P, IC])
        wxp = sb("wxp", [P, IC, STK])
        negA = sb("negA", [P, IC, STATES])
        dpar = sb("dpar", [P, IC])
        dtw = sb("dtw", [P, IC])
        dtb = sb("dtb", [P, IC])
        wout = sb("wout", [P, IC, D])
        lng = sb("lng", [P, IC])
        lnb = sb("lnb", [P, IC])
        wr = sb("wr", [P, DC, D])
        wk = sb("wk", [P, DC, D])
        wv = sb("wv", [P, DC, D])
        mur = sb("mur", [P, DC])
        muk = sb("muk", [P, DC])
        omr = sb("omr", [P, DC])
        omk = sb("omk", [P, DC])
        wqk = sb("wqk", [P, DC, 2 * QK])
        bq = sb("bq", [QK, 1])
        bk = sb("bk", [QK, 1])
        wvv = sb("wvv", [P, DC, D])
        bv = sb("bv", [TB, D])
        gam = sb("gam", [TB, 1])
        wg = sb("wg", [P, DC, EXPERTS])
        bg = sb("bg", [TB, BLK, EXPERTS])
        we = sb("we", [P, DC, EXPERTS * D])
        be = sb("be", [EXPERTS, D])
        idn = sb("idn", [P, P])
        selF = sb("selF", [STK, PROJ])
        sel = sb("sel", [STK, PROJ], BF16)
        spl = sb("spl", [STK, 2])
        hm = sb("hm", [QK, HEADS])
        rk = sb("rk", [TB, BLK, EXPERTS])
        epsc = sb("epsc", [TB, BLK])
        mhalf = sb("mhalf", [TB, BLK])

        xin = sb("xin", [CROWS, ROWS * WIDTH])
        px = sb("px", [CROWS, SIDE, ROWS, PATCH])
        patT = sb("patT", [P, HALVES * SIDE, CROWS])
        hT = [sb(f"hT{i}", [P, DC, T]) for i in range(2)]
        hK = [sb(f"hK{i}", [P, DC, T]) for i in range(2)]
        xpad = sb("xpad", [P, IC, TAPS - 1 + T])
        xbs = sb("xbs", [P, IC, T])
        pj = sb("pj", [STK, T])
        pj1 = sb("pj1", [STK, T])
        hi1 = sb("hi1", [STK, T], BF16)
        hi2 = sb("hi2", [STK, T], BF16)
        stack = sb("stack", [STK, T], BF16)
        dtin = sb("dtin", [P, T])
        soft = sb("soft", [P, IC, T])
        dt_ = [sb(f"dt{i}", [P, IC, T]) for i in range(2)]
        u = [sb(f"u{i}", [P, IC, T]) for i in range(2)]
        xD = [sb(f"xD{i}", [P, IC, T]) for i in range(2)]
        Bb = sb("Bb", [P, STATES, T])
        Cb = sb("Cb", [P, STATES, T])
        dA = [sb(f"dA{i}", [P, NG, T]) for i in range(DRING)]
        X = [sb(f"X{i}", [P, NG, T]) for i in range(RING)]
        ysb = sb("ysb", [TB, BLK, INNER])
        zs = sb("zs", [P, IC, T])
        y3 = sb("y3", [P, IC, T])
        h1 = sb("h1", [TB, BLK, D])
        h1T = sb("h1T", [P, DC, 1 + T])
        xr = sb("xr", [P, DC, T])
        xk = sb("xk", [P, DC, T])
        rs = sb("rs", [TB, BLK, D])
        ka = sb("ka", [P, DC, T])
        h2 = [sb(f"h2{i}", [TB, BLK, D]) for i in range(2)]
        h2T = sb("h2T", [P, DC, T])
        qs = sb("qs", [QK, T])
        ks = sb("ks", [QK, T])
        qm = sb("qm", [QK, HEADS, T])
        vs = [sb(f"vs{i}", [TB, BLK, D]) for i in range(2)]
        pr = [sb(f"pr{i}", [TB, HU, T]) for i in range(2)]
        pT = sb("pT", [TB, 2, 2 * T])
        nmx = [sb(f"nmx{i}", [TB, HU]) for i in range(2)]
        sums = [sb(f"sums{i}", [TB, HU]) for i in range(2)]
        rg = sb("rg", [TB, HU])
        att = sb("att", [TB, BLK, D])
        h3 = sb("h3", [TB, BLK, D])
        h3T = [sb(f"h3T{i}", [P, DC, T]) for i in range(2)]
        acc = sb("acc", [TB, BLK, D])
        ob = sb("ob", [TB, BLK, D])
        gl = sb("gl", [TB, BLK, EXPERTS])
        gw = sb("gw", [TB, BLK, EXPERTS])
        g2 = sb("g2", [TB, BLK, EXPERTS])
        oh1 = sb("oh1", [TB, BLK, EXPERTS])
        oh2 = sb("oh2", [TB, BLK, EXPERTS])
        gs = sb("gs", [TB, 6, BLK])
        wsT = sb("wsT", [EXPERTS, T])
        LN = ("y", "out", "ffn", "att", "moe")
        stat = {n: sb(f"stat_{n}", [TB, BLK, 6]) for n in LN}
        mv = {n: sb(f"mv_{n}", [TB, BLK, 2]) for n in LN}
        veps = {n: sb(f"veps_{n}", [TB, BLK]) for n in LN}
        rstd = {n: sb(f"rstd_{n}", [TB, BLK]) for n in LN}

        FB = psum("FB", [P, 2, 512])
        AB = psum("AB", [P, 2, 512])
        SB = psum("SB", [P, 2, 512])
        MB = psum("MB", [P, 512])
        YB = psum("YB", [P, 512])

        def bank(name, tile, uses):
            return Bank(tile, uses, sem(f"{name}_filled"), sem(f"{name}_drained"))

        F0, F1 = bank("f0", FB[:, 0, :], F0_USES), bank("f1", FB[:, 1, :], F1_USES)
        A0, A1 = bank("a0", AB[:, 0, :], A0_USES), bank("a1", AB[:, 1, :], A1_USES)
        S = bank("s", SB[0:TB, :, 0:2 * T], S_USES)
        M = bank("m", MB[:], M_USES)
        PAIR_BANK = (M, A1, M, A0, A1, M, A0, M)

        x_landed = sem("x_landed")
        w_landed = sem("w_landed")
        out_landed = sem("out_landed")
        reordered = sem("reordered")
        const_ready = sem("const_ready")
        nega_exp = sem("nega_exp")
        zeros_ready = sem("zeros_ready")
        conv_step = sem("conv_step")
        tanh_x = sem("tanh_x")
        x_ready = sem("x_ready")
        xD_ready = sem("xD_ready")
        split_step = sem("split_step")
        soft_step = sem("soft_step")
        dt_ready = sem("dt_ready")
        u_ready = sem("u_ready")
        dA_ready = sem("dA_ready")
        xs_dve = sem("xs_dve")
        xs_pool = sem("xs_pool")
        scan_done = sem("scan_done")
        prod_ready = sem("prod_ready")
        folded = sem("folded")
        prod_used = sem("prod_used")
        h_kept = sem("h_kept")
        tanh_z = sem("tanh_z")
        y_drained = sem("y_drained")
        stats_step = {n: sem(f"stats_{n}") for n in LN}
        rstd_step = {n: sem(f"rstd_{n}") for n in LN}
        normed = {n: sem(f"normed_{n}") for n in LN}
        y3_ready = sem("y3_ready")
        before_step = sem("before_step")
        mix_step = sem("mix_step")
        ksq_ready = sem("ksq_ready")
        ffn_sum_done = sem("ffn_sum_done")
        qm_ready = sem("qm_ready")
        leaky_ready = sem("leaky_ready")
        nmx_ready = sem("nmx_ready")
        pr_ready = sem("pr_ready")
        av_step = sem("av_step")
        att_sum = sem("att_sum")
        gate_step = sem("gate_step")
        gate_exp = sem("gate_exp")
        moe_step = sem("moe_step")
        dve_past = sem("dve_past")
        pe_past = sem("pe_past")

        def made_by(g):
            return (xs_pool, POOL_INPUTS) if g in POOL_INPUTS else (xs_dve, DVE_INPUTS)

        flat = x.rearrange("(b r) n -> b r n", r=CROWS)
        out_v = out.rearrange("(b k p) d -> b p k d", k=BLK, p=TB)
        loads = [(wtok, w_tok), (btok, b_tok), (win, w_in), (cw, conv_w), (cb, conv_b), (wxp, w_xproj),
                 (negA, a_log), (dpar, d_par), (dtw, dt_w), (dtb, dt_b), (wout, w_out), (lng, ln_g), (lnb, ln_b),
                 (wr, w_r), (wk, w_k), (wv, w_v), (mur, mu_r), (muk, mu_k), (wqk, w_qk), (bq, b_q),
                 (bk, b_k), (wvv, w_vv), (bv, b_v), (gam, gamma), (wg, w_g), (bg, b_g), (we, w_e), (be, b_e),
                 (idn, ident), (selF, select), (spl, split_masks), (hm, head_mask), (rk, rank_of)]
        W_ALL = 16 * len(loads)
        CONSTS = 9

        def schedule(eng, step):
            for b in range(FIRST, LOOP_FROM):
                step(b, b % 2)
            with eng.Fori(0, LOOP_PAIRS) as pair:
                b = pair * 2
                step(b + LOOP_FROM, LOOP_FROM % 2)
                step(b + (LOOP_FROM + 1), (LOOP_FROM + 1) % 2)
            for b in range(LOOP_FROM + 2 * LOOP_PAIRS, LAST + 1):
                step(b, b % 2)

        block = ctx.enter_context(nc.Block())

        @block.sync
        def _(sp):
            def load(s, h):
                if isinstance(s, int) and not 0 <= s < IMAGES:
                    return
                after(sp, reordered, HALVES * s + h)
                src = flat[s, :, :] if isinstance(s, int) else flat[bass.ds(s, 1), :, :].rearrange("a r n -> (a r) n")
                sp.dma_start(xin[:], src[:, h * ROWS * WIDTH:(h + 1) * ROWS * WIDTH]).then_inc(x_landed, 16)

            def step(b, par):
                load(b - FIRST, 1)
                load(b - FIRST + 1, 0)
                s = image_of(b, AT_MOE_NORM)
                if not isinstance(s, int) or s >= 0:
                    sp.wait_ge(normed["moe"], s + 1)
                    dst = out_v[s] if isinstance(s, int) else \
                        out_v[bass.ds(s, 1)].rearrange("a p k d -> (a p) k d")
                    sp.dma_start(dst, ob[:]).then_inc(out_landed, 16)

            load(0, 0)
            for dst, src in loads:
                sp.dma_start(dst[:], src).then_inc(w_landed, 16)
            schedule(sp, step)
            sp.wait_ge(out_landed, 16 * IMAGES)

        @block.gpsimd
        def _(pool):
            tt = nc.gpsimd.tensor_tensor

            def make_u(s, q):
                pool.wait_ge(dt_ready, s + 1)
                after(pool, xs_dve, len(DVE_INPUTS) * (s - 1))
                after(pool, xs_pool, len(POOL_INPUTS) * (s - 1))
                tt(u[q][:], dt_[q][:], xbs[:], ALU.mult).then_inc(u_ready, 1)

            def inputs(s, q, g):
                c, ng = g // GC, g % GC
                if g == POOL_INPUTS[0]:
                    pool.wait_ge(u_ready, s + 1)
                if c == 0 or ng not in [x % GC for x in POOL_INPUTS if x < g]:
                    pool.wait_ge(F1.drained, F1.count(f"B{ng}", s))
                after(pool, prod_used, GROUPS * s + g + 1 - RING)
                tt(X[g % RING][:], u[q][:, c:c + 1, :].broadcast_to([P, NG, T]), Bb[:, NG * ng:NG * (ng + 1), :],
                   ALU.mult).then_inc(xs_pool, 1)

            def times_c(s, g):
                pool.wait_ge(scan_done, GROUPS * s + g + 1)
                if g < GC:
                    pool.wait_ge(F1.drained, F1.count(f"C{g}", s))
                t = X[g % RING]
                n0 = NG * (g % GC)
                tt(t[:], t[:], Cb[:, n0:n0 + NG, :], ALU.mult).then_inc(prod_ready, 1)

            def inverse_std(s, n):
                pool.wait_ge(stats_step[n], 4 * (s + 1))
                tt(veps[n][:], mv[n][:, :, 1], epsc[:], ALU.add).then_inc(rstd_step[n], 1)
                pool.wait_ge(rstd_step[n], 2 * s + 1)
                tt(rstd[n][:], veps[n][:], mhalf[:], ALU.pow).then_inc(rstd_step[n], 1)

            def step(b, par):
                for g in range(GROUPS):
                    def at(slot):
                        return live(b, par, g, slot)

                    for n, slot in (("y", AT_Y_STD), ("out", AT_OUT_STD), ("ffn", AT_FFN_STD), ("att", AT_ATT_STD),
                                    ("moe", AT_MOE_STD)):
                        for s, q in at(slot):
                            inverse_std(s, n)
                    for s, q in at(AT_Y3):
                        pool.wait_ge(A1.drained, A1.count("turn_y", s))
                        pool.wait_ge(F1.drained, F1.count("z", s))
                        tt(y3[:], y3[:], zs[:], ALU.mult).then_inc(y3_ready, 1)
                    for s, q in at(AT_U):
                        make_u(s, q)
                    for k in POOL_INPUTS:
                        for s, q in at(k - 1):
                            inputs(s, q, k)
                    for s, q in at(AT_KSQ):
                        pool.wait_ge(A1.drained, A1.count("k", s))
                        tt(ka[:], ka[:], ka[:], ALU.mult).then_inc(ksq_ready, 1)
                    for k in range(GROUPS):
                        for s, q in at(k + 1):
                            times_c(s, k)

            nc.gpsimd.memset(xpad[:, :, 0:TAPS - 1], 0.0)
            nc.gpsimd.memset(h1T[:, :, 0:1], 0.0)
            nc.gpsimd.memset(epsc[:], LN_EPS).then_inc(zeros_ready, 1)
            nc.gpsimd.memset(mhalf[:], -0.5).then_inc(zeros_ready, 1)
            for i in range(DRING):
                last = nc.gpsimd.memset(dA[i][:, :, 0:1], 0.0)
            last.then_inc(zeros_ready, 1)
            pool.wait_ge(zeros_ready, 3)
            schedule(pool, step)

        @block.tensor
        def _(pe):
            mm = nc.tensor.matmul

            def free(bank, name, s):
                after(pe, bank.drained, bank.count(name, s) - 1)
                return bank.tile

            def patches(s, h):
                pe.wait_ge(reordered, HALVES * s + h + 1)
                for f, bank in enumerate((F0, F1)):
                    o = free(bank, f"patch{h}", s)
                    pe.sem_inc(pe_past, 1)
                    for i in range(SIDE // 2):
                        last = nc.tensor.transpose(o[:, i * CROWS:(i + 1) * CROWS],
                                                   px[:, f * SIDE // 2 + i, :, :].rearrange("r p w -> r (p w)"),
                                                   idn[:CROWS, :CROWS])
                    last.then_inc(bank.filled, 1)

            def embed(s):
                pe.wait_ge(F1.drained, F1.count("patch1", s))
                for m, bank in enumerate((F0, F1)):
                    o = free(bank, "embed", s)
                    for k in range(KP):
                        c, half = k // HALVES, k % HALVES
                        rhs = patT[:, half * SIDE:(half + 1) * SIDE, c * SIDE:(c + 1) * SIDE].rearrange(
                            "p w h -> p h w")
                        last = mm(o[:, 0:T], lhsT=wtok[:, k, m * P:(m + 1) * P], rhs=rhs,
                                  start=(k == 0), stop=(k == KP - 1))
                    last.then_inc(bank.filled, 1)

            def project_in(s, src, name, first_chunk):
                for f, bank in enumerate((F0, F1)):
                    o = free(bank, name, s)
                    for j in range(2):
                        m = first_chunk + 2 * f + j
                        for k in range(DC):
                            last = mm(o[:, j * T:(j + 1) * T], lhsT=win[:, k, m * P:(m + 1) * P], rhs=src[:, k, :],
                                      start=(k == 0), stop=(k == DC - 1))
                    last.then_inc(bank.filled, 1)

            def xproj(s):
                pe.wait_ge(x_ready, s + 1)
                o = free(A1, "xproj", s)
                for k in range(IC):
                    last = mm(o[0:STK, 0:T], lhsT=wxp[:, k, :], rhs=xbs[:, k, :], start=(k == 0), stop=(k == IC - 1))
                last.then_inc(A1.filled, 1)

            def spread(o, row):
                return mm(o, lhsT=sel[:, row:row + 1].broadcast_to([STK, P]), rhs=stack[:], start=True, stop=True)

            def dt_row(s):
                pe.wait_ge(split_step, 4 * s + 4)
                spread(free(F1, "dt", s)[:, 0:T], 0).then_inc(F1.filled, 1)

            def spread_group(s, name, row0):
                for i, bank in enumerate((F0, F1)):
                    o = free(bank, name, s)
                    spread(o[:, 0:T], row0 + 2 * i)
                    spread(o[:, T:2 * T], row0 + 2 * i + 1).then_inc(bank.filled, 1)

            def sum_states(s, q, g):
                c = g // GC
                if g % GC == 0:
                    if c == 0:
                        pe.wait_ge(xD_ready, s + 1)
                    after(pe, y_drained, IC * s + c)
                    for k in range(BLK):
                        mm(YB[0:TB, k * P:(k + 1) * P], lhsT=xD[q][:, c, k * TB:(k + 1) * TB], rhs=idn[:],
                           is_transpose=True, start=(k == 0), stop=False, skip_group_check=True)
                if g in FOLDED:
                    pe.wait_ge(folded, len(FOLDED) * s + rank(FOLDED, g))
                else:
                    pe.wait_ge(prod_ready, GROUPS * s + g + 1)
                states = NG // 2 if g in FOLDED else NG
                for j in range(states):
                    for k in range(BLK):
                        last = mm(YB[0:TB, k * P:(k + 1) * P], lhsT=X[g % RING][:, j, k * TB:(k + 1) * TB],
                                  rhs=idn[:], is_transpose=True, start=False,
                                  stop=(g % GC == GC - 1 and j == states - 1), skip_group_check=True)
                last.then_inc(prod_used, 1)

            def turn_y(s):
                pe.wait_ge(normed["y"], s + 1)
                for i, bank in enumerate((A0, A1)):
                    o = free(bank, "turn_y", s)
                    for j in range(2):
                        c = 2 * i + j
                        for k in range(BLK):
                            last = nc.tensor.transpose(o[:, j * T + k * TB:j * T + (k + 1) * TB],
                                                       ysb[:, k, c * P:(c + 1) * P], idn[:TB, :TB])
                    last.then_inc(bank.filled, 1)

            def project_out(s, q):
                pe.wait_ge(y3_ready, s + 1)
                o = free(A0, "out", s)
                for k in range(BLK):
                    tok = slice(k * TB, (k + 1) * TB)
                    for c in range(IC):
                        mm(o[0:TB, k * D:(k + 1) * D], lhsT=y3[:, c, tok], rhs=wout[:, c, :],
                           start=(k == 0 and c == 0), stop=False, skip_group_check=True)
                    for m in range(DC):
                        last = mm(o[0:TB, k * D + m * P:k * D + (m + 1) * P], lhsT=hK[q][:, m, tok], rhs=idn[:],
                                  is_transpose=True, start=False, stop=(m == DC - 1), skip_group_check=True)
                last.then_inc(A0.filled, 1)

            def turn(s, bank, name, src):
                o = free(bank, name, s)
                for m in range(DC):
                    for k in range(BLK):
                        last = nc.tensor.transpose(o[:, m * T + k * TB:m * T + (k + 1) * TB],
                                                   src[:, k, m * P:(m + 1) * P], idn[:TB, :TB])
                last.then_inc(bank.filled, 1)

            def token_major(s, name, lhs, rhs):
                o = free(A0, name, s)
                for k in range(BLK):
                    for c in range(DC):
                        last = mm(o[0:TB, k * D:(k + 1) * D], lhsT=lhs[:, c, k * TB:(k + 1) * TB], rhs=rhs[:, c, :],
                                  start=(c == 0), stop=(c == DC - 1))
                last.then_inc(A0.filled, 1)

            def mix_keys(s):
                o = free(A1, "k", s)
                for m in range(DC):
                    for k in range(DC):
                        last = mm(o[:, m * T:(m + 1) * T], lhsT=wk[:, k, m * P:(m + 1) * P], rhs=xk[:, k, :],
                                  start=(k == 0), stop=(k == DC - 1))
                last.then_inc(A1.filled, 1)

            def queries_keys(s):
                o = free(A1, "qk", s)
                for k in range(DC):
                    last = mm(o[0:2 * QK, 0:T], lhsT=wqk[:, k, :], rhs=h2T[:, k, :], start=(k == 0),
                              stop=(k == DC - 1))
                last.then_inc(A1.filled, 1)

            def scores(s, n):
                k, h0 = n // 2, HU * (n % 2)
                if n == 0:
                    pe.wait_ge(qm_ready, s + 1)
                o = free(S, f"S{n}", s)
                for j in range(HU):
                    last = mm(o[:, j // 2, (j % 2) * T:(j % 2 + 1) * T], lhsT=qm[:, h0 + j, k * TB:(k + 1) * TB],
                              rhs=ks[:], start=True, stop=True)
                last.then_inc(S.filled, 1)

            def turn_probs(s, n):
                pe.wait_ge(pr_ready, UNITS * s + n + 1)
                o = free(S, f"P{n}", s)
                for j in range(HU):
                    for k in range(BLK):
                        at = ((j % 2) * 2 + k) * TB
                        last = nc.tensor.transpose(o[:, j // 2, at:at + TB], pr[n % 2][:, j, k * TB:(k + 1) * TB],
                                                   idn[:TB, :TB])
                last.then_inc(S.filled, 1)

            def mix_values(s, q, n):
                h0 = HU * (n % 2)
                pe.wait_ge(S.drained, S.count(f"P{n}", s))
                if n == 0:
                    pe.wait_ge(A0.drained, A0.count("values", s))
                o = free(M, f"AV{n}", s)
                for j in range(HU):
                    for k in range(BLK):
                        at = ((j % 2) * 2 + k) * TB
                        last = mm(o[0:TB, j * DV:(j + 1) * DV], lhsT=pT[:, j // 2, at:at + TB],
                                  rhs=vs[q][:, k, (h0 + j) * DV:(h0 + j + 1) * DV], start=(k == 0),
                                  stop=(k == BLK - 1))
                last.then_inc(M.filled, 1)

            def gate(s, q):
                pe.wait_ge(A0.drained, A0.count("h3T", s))
                o = free(M, "gate", s)
                for k in range(BLK):
                    for c in range(DC):
                        last = mm(o[0:TB, k * EXPERTS:(k + 1) * EXPERTS], lhsT=h3T[q][:, c, k * TB:(k + 1) * TB],
                                  rhs=wg[:, c, :], start=(c == 0), stop=(c == DC - 1))
                last.then_inc(M.filled, 1)

            def expert_pair(s, q, m):
                pair, k = m // 2, m % 2
                bank = PAIR_BANK[m]
                o = free(bank, f"pair{m}", s)
                for c in range(DC):
                    last = mm(o[0:TB, :], lhsT=h3T[q][:, c, k * TB:(k + 1) * TB],
                              rhs=we[:, c, pair * 2 * D:(pair + 1) * 2 * D], start=(c == 0), stop=(c == DC - 1))
                last.then_inc(bank.filled, 1)

            def turn_gates(s):
                pe.wait_ge(gate_step, GSTEPS * (s + 1))
                o = free(A0, "ws", s)
                for k in range(BLK):
                    last = nc.tensor.transpose(o[0:EXPERTS, k * TB:(k + 1) * TB], gw[:, k, :], idn[:TB, :TB])
                last.then_inc(A0.filled, 1)

            def expert_biases(s):
                o = free(F0, "be", s)
                pe.wait_ge(A0.drained, A0.count("ws", s))
                for k in range(BLK):
                    last = mm(o[0:TB, k * D:(k + 1) * D], lhsT=wsT[:, k * TB:(k + 1) * TB], rhs=be[:],
                              start=True, stop=True)
                last.then_inc(F0.filled, 1)

            def step(b, par):
                for g in range(GROUPS):
                    def at(slot):
                        return live(b, par, g, slot)

                    for s, q in at(AT_VALUES):
                        token_major(s, "values", h2T, wvv)
                    for s, q in at(AT_GATE):
                        gate(s, q)
                    for s, q in at(AT_EMBED):
                        embed(s)
                    for s, q in at(AT_XPROJ):
                        xproj(s)
                    for s, q in at(AT_WS):
                        turn_gates(s)
                    for s, q in at(AT_TURN_Y):
                        turn_y(s)
                    for s, q in at(AT_QK):
                        queries_keys(s)
                    for m in range(PAIRS):
                        for s, q in at(AT_PAIR[m]):
                            expert_pair(s, q, m)
                    for s, q in at(AT_V):
                        pe.wait_ge(ksq_ready, s + 1)
                        token_major(s, "v", ka, wv)
                    for h in range(HALVES):
                        for s, q in at(AT_PATCH[h]):
                            patches(s, h)
                    for s, q in at(AT_RK):
                        pe.wait_ge(mix_step, 4 * (s + 1))
                        token_major(s, "r", xr, wr)
                        mix_keys(s)
                    for n in range(UNITS):
                        for s, q in at(AT_SCORES[n]):
                            scores(s, n)
                        for s, q in at(AT_TURN_P[n]):
                            turn_probs(s, n)
                        for s, q in at(AT_AV[n]):
                            mix_values(s, q, n)
                    for s, q in at(AT_Z):
                        pe.wait_ge(h_kept, s + 1)
                        project_in(s, hK[q], "z", IC)
                    for s, q in at(AT_DT):
                        dt_row(s)
                    for s, q in at(AT_H1T):
                        pe.wait_ge(A0.drained, A0.count("out", s))
                        turn(s, A1, "h1T", h1)
                    for k in range(GROUPS):
                        for s, q in at(k + 2):
                            sum_states(s, q, k)
                    for s, q in at(AT_BE):
                        expert_biases(s)
                    for s, q in at(AT_XB):
                        pe.wait_ge(F1.drained, F1.count("embed", s))
                        project_in(s, hT[q], "xb", 0)
                    for s, q in at(AT_H2T):
                        pe.wait_ge(normed["ffn"], s + 1)
                        turn(s, A1, "h2T", h2[q])
                    for s, q in at(AT_H3T):
                        pe.wait_ge(normed["att"], s + 1)
                        turn(s, A0, "h3T", h3)
                    for ng in range(GC):
                        for s, q in at(AT_B[ng]):
                            spread_group(s, f"B{ng}", 1 + NG * ng)
                        for s, q in at(AT_C[ng]):
                            spread_group(s, f"C{ng}", 1 + STATES + NG * ng)
                    for s, q in at(AT_OUT):
                        project_out(s, q)

            pe.wait_ge(w_landed, W_ALL)
            pe.wait_ge(const_ready, CONSTS)
            schedule(pe, step)

        @block.scalar
        def _(act):
            go = nc.scalar.activation

            def filled(bank, name, s):
                act.wait_ge(bank.filled, bank.count(name, s))
                return bank.tile

            def drain_patches(s, h):
                for f, bank in enumerate((F0, F1)):
                    o = filled(bank, f"patch{h}", s)
                    q0 = h * SIDE + f * SIDE // 2
                    go(patT[:, q0:q0 + SIDE // 2, :], o[:, 0:SIDE // 2 * CROWS].rearrange("p (q r) -> p q r", r=CROWS),
                       ACT.Copy).then_inc(bank.drained, 1)

            def drain_embed(s, q):
                after(act, h_kept, s - 1)
                for m, bank in enumerate((F0, F1)):
                    o = filled(bank, "embed", s)
                    go(hT[q][:, m, :], o[:, 0:T], ACT.Identity, bias=btok[:, m:m + 1]).then_inc(bank.drained, 1)

            def drain_xb(s):
                after(act, conv_step, TAPS * IC * s)
                for f, bank in enumerate((F0, F1)):
                    o = filled(bank, "xb", s)
                    go(xpad[:, 2 * f:2 * f + 2, TAPS - 1:], o[:, 0:2 * T].rearrange("p (c t) -> p c t", c=2),
                       ACT.Copy).then_inc(bank.drained, 1)

            def tanh_of_z(s):
                after(act, y3_ready, s)
                filled(F0, "z", s)
                filled(F1, "z", s)
                go(zs[:].rearrange("p (a b) t -> p a (b t)", a=2), FB[:, :, 0:2 * T], ACT.Tanh,
                   scale=0.5).then_inc(tanh_z, 1)

            def tanh_of_x(s):
                act.wait_ge(conv_step, TAPS * IC * (s + 1))
                after(act, dt_ready, s)
                go(soft[:], xbs[:], ACT.Tanh).then_inc(tanh_x, 1)

            def times_d(s, q):
                act.wait_ge(x_ready, s + 1)
                after(act, prod_used, GROUPS * (s - 1) - GC + 1)
                for c in range(IC):
                    last = go(xD[q][:, c, :], xbs[:, c, :], ACT.Copy, scale=dpar[:, c:c + 1])
                last.then_inc(xD_ready, 1)

            def drain_proj(s):
                o = filled(A1, "xproj", s)
                after(act, split_step, 4 * s)
                go(pj[:], o[0:STK, 0:T], ACT.Copy).then_inc(A1.drained, 1)

            def drain_dt(s):
                o = filled(F1, "dt", s)
                after(act, soft_step, 3 * s)
                go(dtin[:], o[:, 0:T], ACT.Copy).then_inc(F1.drained, 1)

            def softplus(s, q):
                act.wait_ge(F1.drained, F1.count("dt", s))
                act.wait_ge(x_ready, s + 1)
                after(act, u_ready, s - 1)
                for c in range(IC):
                    go(dt_[q][:, c, :], dtin[:], ACT.Relu, scale=dtw[:, c:c + 1], bias=dtb[:, c:c + 1])
                for c in range(IC):
                    last = go(soft[:, c, :], dtin[:], ACT.Abs, scale=dtw[:, c:c + 1], bias=dtb[:, c:c + 1])
                last.then_inc(soft_step, 1)
                act.wait_ge(soft_step, 3 * s + 1)
                go(soft[:], soft[:], ACT.Exp, scale=-1.0).then_inc(soft_step, 1)
                act.wait_ge(soft_step, 3 * s + 2)
                go(soft[:], soft[:], ACT.Ln, bias=1.0).then_inc(soft_step, 1)

            def drain_group(s, name, dst, ng):
                for i, bank in enumerate((F0, F1)):
                    o = filled(bank, name, s)
                    n0 = NG * ng + 2 * i
                    go(dst[:, n0:n0 + 2, :], o[:, 0:2 * T].rearrange("p (c t) -> p c t", c=2),
                       ACT.Copy).then_inc(bank.drained, 1)

            def decay(s, q, g):
                c = g // GC
                if g == 0:
                    act.wait_ge(dt_ready, s + 1)
                after(act, scan_done, GROUPS * s + g + 1 - DRING)
                for j in range(NG):
                    n = NG * (g % GC) + j
                    last = go(dA[g % DRING][:, j, 1:T], dt_[q][:, c, 1:T], ACT.Exp, scale=negA[:, c, n:n + 1])
                last.then_inc(dA_ready, 1)

            def drain_y(s, c):
                act.wait_ge(prod_used, GROUPS * s + GC * (c + 1))
                if c == 0 and not (isinstance(s, int) and s == 0):
                    act.wait_ge(A1.filled, A1.count("turn_y", s - 1))
                go(ysb[:, :, c * P:(c + 1) * P], YB[0:TB, 0:BLK * P].rearrange("p (k d) -> p k d", k=BLK),
                   ACT.Copy).then_inc(y_drained, 1)

            def scale_y(s):
                for i, bank in enumerate((A0, A1)):
                    o = filled(bank, "turn_y", s)
                    for j in range(2):
                        c = 2 * i + j
                        last = go(y3[:, c, :], o[:, j * T:(j + 1) * T], ACT.Identity, scale=lng[:, c:c + 1],
                                  bias=lnb[:, c:c + 1])
                    last.then_inc(bank.drained, 1)

            def drain_turned(s, bank, name, dst):
                o = filled(bank, name, s)
                go(dst, o[:, 0:DC * T].rearrange("p (c t) -> p c t", c=DC), ACT.Copy).then_inc(bank.drained, 1)

            def tokens_before(s):
                act.wait_ge(A1.drained, A1.count("h1T", s))
                for dst, om in ((xr, omr), (xk, omk)):
                    for m in range(DC):
                        go(dst[:, m, :], h1T[:, m, 0:T], ACT.Copy, scale=om[:, m:m + 1]).then_inc(before_step, 1)

            def drain_rk(s):
                o = filled(A0, "r", s)
                after(act, normed["ffn"], s)
                go(rs[:], o[0:TB, :].rearrange("p (k d) -> p k d", k=BLK), ACT.Tanh, scale=0.5).then_inc(A0.drained, 1)
                o = filled(A1, "k", s)
                go(ka[:], o[:, 0:DC * T].rearrange("p (c t) -> p c t", c=DC), ACT.Relu).then_inc(A1.drained, 1)

            def drain_qk(s):
                o = filled(A1, "qk", s)
                if not (isinstance(s, int) and s == 0):
                    act.wait_ge(S.filled, S.count(f"S{UNITS - 1}", s - 1))
                    act.wait_ge(qm_ready, s)
                go(qs[:], o[0:QK, 0:T], ACT.Identity, bias=bq[:])
                go(ks[:], o[QK:2 * QK, 0:T], ACT.Identity, bias=bk[:]).then_inc(A1.drained, 1)

            def drain_scores(s, n):
                o = filled(S, f"S{n}", s)
                go(pr[n % 2][:].rearrange("p (a b) t -> p a (b t)", a=2), o, ACT.Copy).then_inc(S.drained, 1)

            def probs(s, n):
                act.wait_ge(nmx_ready, UNITS * s + n + 1)
                if not (isinstance(s, int) and s == 0 and n < 2):
                    act.wait_ge(av_step, 2 * (UNITS * s + n - 1))
                for j in range(HU):
                    last = go(pr[n % 2][:, j, :], pr[n % 2][:, j, :], ACT.Exp, bias=nmx[n % 2][:, j:j + 1],
                              accum_out=sums[n % 2][:, j:j + 1])
                last.then_inc(pr_ready, 1)

            def drain_pT(s, n):
                o = filled(S, f"P{n}", s)
                go(pT[:], o, ACT.Copy).then_inc(S.drained, 1)

            def step(b, par):
                for g in range(GROUPS):
                    def at(slot):
                        return live(b, par, g, slot)

                    for s, q in at(AT_H2T_OUT):
                        drain_turned(s, A1, "h2T", h2T[:])
                    for s, q in at(AT_XB_OUT):
                        drain_xb(s)
                    for s, q in at(AT_XD):
                        times_d(s, q)
                    for h in range(HALVES):
                        for s, q in at(AT_PATCH_OUT[h]):
                            drain_patches(s, h)
                    for n in range(UNITS):
                        for s, q in at(AT_TURN_P[n] + 1):
                            drain_pT(s, n)
                        for s, q in at(AT_SCORES[n] + 1):
                            drain_scores(s, n)
                    for s, q in at(AT_H3T_OUT):
                        drain_turned(s, A0, "h3T", h3T[q][:])
                    for s, q in at(AT_XPROJ_OUT):
                        drain_proj(s)
                    for s, q in at(AT_DT_OUT):
                        drain_dt(s)
                    for s, q in at(AT_H1T_OUT):
                        after(act, mix_step, 4 * s)
                        drain_turned(s, A1, "h1T", h1T[:, :, 1:])
                        tokens_before(s)
                    for s, q in at(AT_QK_OUT):
                        drain_qk(s)
                    for s, q in at(AT_GATE_EXP):
                        act.wait_ge(gate_step, GSTEPS * s + GIN)
                        go(gl[:], gl[:], ACT.Exp).then_inc(gate_exp, 1)
                    for s, q in at(AT_YG):
                        scale_y(s)
                    for s, q in at(AT_WS_OUT):
                        o = filled(A0, "ws", s)
                        go(wsT[:], o[0:EXPERTS, 0:T], ACT.Copy).then_inc(A0.drained, 1)
                    for s, q in at(AT_RK_OUT):
                        drain_rk(s)
                    for k in range(GROUPS):
                        for s, q in at(k - 1):
                            decay(s, q, k)
                    for n in range(UNITS):
                        for s, q in at(AT_SCORES[n] + 3):
                            probs(s, n)
                    for c in range(IC):
                        for s, q in at(AT_Y_OUT[c]):
                            drain_y(s, c)
                    for ng in range(GC):
                        for s, q in at(AT_B[ng] + 1):
                            made, groups = made_by(GROUPS - GC + ng)
                            after(act, made, len(groups) * s - len(groups) + rank(groups, GROUPS - GC + ng))
                            drain_group(s, f"B{ng}", Bb, ng)
                        for s, q in at(AT_C[ng] + 1):
                            after(act, prod_ready, GROUPS * s - GC + ng + 1)
                            drain_group(s, f"C{ng}", Cb, ng)
                    for s, q in at(AT_TANH_X):
                        tanh_of_x(s)
                    for s, q in at(AT_EMBED_OUT):
                        drain_embed(s, q)
                    for s, q in at(AT_Z_OUT):
                        tanh_of_z(s)
                    for s, q in at(AT_DT_OUT):
                        softplus(s, q)

            act.wait_ge(w_landed, W_ALL)
            go(negA[:], negA[:], ACT.Exp).then_inc(nega_exp, 1)
            act.wait_ge(zeros_ready, 3)
            act.wait_ge(const_ready, CONSTS)
            schedule(act, step)

        @block.vector
        def _(dve):
            v = nc.vector

            def reorder(s, h):
                dve.wait_ge(x_landed, 16 * (HALVES * s + h + 1))
                if h == 1:
                    dve.wait_ge(F1.filled, F1.count("patch0", s))
                elif not (isinstance(s, int) and s == 0):
                    dve.wait_ge(F1.filled, F1.count("patch1", s - 1))
                v.tensor_copy(px[:], xin[:].rearrange("r (p q w) -> r q p w", p=ROWS, w=PATCH)).then_inc(reordered, 1)

            def taps(s, which):
                if which[0] == 0:
                    after(dve, u_ready, s)
                    after(dve, xD_ready, s)
                    if not (isinstance(s, int) and s == 0):
                        dve.wait_ge(A1.filled, A1.count("xproj", s - 1))
                    dve.wait_ge(F1.drained, F1.count("xb", s))
                for k in which:
                    for c in range(IC):
                        if k == 0:
                            v.tensor_scalar(xbs[:, c, :], xpad[:, c, 0:T], cw[:, c, 0:1], cb[:, c:c + 1],
                                            ALU.mult, ALU.add).then_inc(conv_step, 1)
                        else:
                            dve.wait_ge(conv_step, TAPS * IC * s + IC * (k - 1) + c + 1)
                            v.scalar_tensor_tensor(out=xbs[:, c, :], in0=xpad[:, c, k:k + T],
                                                   scalar=cw[:, c, k:k + 1], in1=xbs[:, c, :], op0=ALU.mult,
                                                   op1=ALU.add).then_inc(conv_step, 1)

            def gate_x(s):
                dve.wait_ge(tanh_x, s + 1)
                v.scalar_tensor_tensor(out=xbs[:], in0=soft[:], scalar=1.0, in1=xbs[:], op0=ALU.add,
                                       op1=ALU.mult).then_inc(x_ready, 1)

            def gate_z(s):
                dve.wait_ge(tanh_z, s + 1)
                for f, bank in enumerate((F0, F1)):
                    v.scalar_tensor_tensor(out=zs[:, 2 * f:2 * f + 2, :], in0=zs[:, 2 * f:2 * f + 2, :], scalar=1.0,
                                           in1=bank.tile[:, 0:2 * T].rearrange("p (c t) -> p c t", c=2), op0=ALU.add,
                                           op1=ALU.mult).then_inc(bank.drained, 1)

            def split(s):
                dve.wait_ge(A1.drained, A1.count("xproj", s))
                if not (isinstance(s, int) and s == 0):
                    dve.wait_ge(F1.filled, F1.count(f"C{GC - 1}", s - 1))
                v.tensor_copy(hi1[:], pj[:]).then_inc(split_step, 1)
                dve.wait_ge(split_step, 4 * s + 1)
                v.scalar_tensor_tensor(out=pj1[:], in0=hi1[:], scalar=spl[:, 0:1], in1=pj[:], op0=ALU.mult,
                                       op1=ALU.add).then_inc(split_step, 1)
                dve.wait_ge(split_step, 4 * s + 2)
                v.tensor_copy(hi2[:], pj1[:]).then_inc(split_step, 1)
                dve.wait_ge(split_step, 4 * s + 3)
                v.scalar_tensor_tensor(out=stack[:], in0=hi2[:], scalar=spl[:, 1:2], in1=pj1[:], op0=ALU.mult,
                                       op1=ALU.add).then_inc(split_step, 1)

            def step_size(s, q):
                dve.wait_ge(soft_step, 3 * (s + 1))
                v.tensor_tensor(dt_[q][:], dt_[q][:], soft[:], ALU.add).then_inc(dt_ready, 1)

            def inputs(s, q, g):
                c, ng = g // GC, g % GC
                if g == DVE_INPUTS[0]:
                    dve.wait_ge(u_ready, s + 1)
                if c == 0 or ng not in [x % GC for x in DVE_INPUTS if x < g]:
                    dve.wait_ge(F1.drained, F1.count(f"B{ng}", s))
                after(dve, prod_used, GROUPS * s + g + 1 - RING)
                v.tensor_tensor(X[g % RING][:], u[q][:, c:c + 1, :].broadcast_to([P, NG, T]),
                                Bb[:, NG * ng:NG * (ng + 1), :], ALU.mult).then_inc(xs_dve, 1)

            def scan_group(s, g):
                made, groups = made_by(g)
                dve.wait_ge(made, len(groups) * s + rank(groups, g))
                dve.wait_ge(dA_ready, GROUPS * s + g + 1)
                t = X[g % RING][:].rearrange("p n t -> p (n t)")
                v.tensor_tensor_scan(t, dA[g % DRING][:].rearrange("p n t -> p (n t)"), t, 0.0, ALU.mult,
                                     ALU.add).then_inc(scan_done, 1)

            def fold_states(s, g):
                dve.wait_ge(prod_ready, GROUPS * s + g + 1)
                t = X[g % RING]
                v.tensor_tensor(t[:, 0:NG // 2, :], t[:, 0:NG // 2, :], t[:, NG // 2:, :],
                                ALU.add).then_inc(folded, 1)

            def moments(s, n, src):
                for k in range(BLK):
                    v.bn_stats(stat[n][:, k, :], src(k)).then_inc(stats_step[n], 1)
                dve.wait_ge(stats_step[n], 4 * s + BLK)
                dve.sem_inc(dve_past, 1)
                for k in range(BLK):
                    v.bn_aggr(mv[n][:, k, :], stat[n][:, k, :]).then_inc(stats_step[n], 1)

            def normalise(s, n, src, dst, done):
                dve.wait_ge(rstd_step[n], 2 * (s + 1))
                for k in range(BLK):
                    last = v.tensor_scalar(dst[:, k, :], src(k), mv[n][:, k, 0:1], rstd[n][:, k:k + 1], ALU.subtract,
                                           ALU.mult)
                last.then_inc(done, 1)

            def token_mix(s):
                for i, (dst, mu) in enumerate(((xr, mur), (xk, muk))):
                    for m in range(DC):
                        dve.wait_ge(before_step, 4 * s + 2 * i + m + 1)
                        v.scalar_tensor_tensor(out=dst[:, m, :], in0=h1T[:, m, 1:], scalar=mu[:, m:m + 1],
                                               in1=dst[:, m, :], op0=ALU.mult, op1=ALU.add).then_inc(mix_step, 1)

            def ffn_sum(s):
                dve.wait_ge(A0.filled, A0.count("v", s))
                v.scalar_tensor_tensor(out=rs[:], in0=rs[:], scalar=1.0,
                                       in1=A0.tile[0:TB, :].rearrange("p (k d) -> p k d", k=BLK), op0=ALU.add,
                                       op1=ALU.mult).then_inc(A0.drained, 1)
                dve.wait_ge(A0.drained, A0.count("v", s))
                v.tensor_tensor(rs[:], rs[:], h1[:], ALU.add).then_inc(ffn_sum_done, 1)

            def heads(s):
                dve.wait_ge(A1.drained, A1.count("qk", s))
                for h in range(HEADS):
                    last = v.tensor_scalar(qm[:, h, :], qs[:], hm[:, h:h + 1], None, ALU.mult)
                last.then_inc(qm_ready, 1)

            def add_value_bias(s, q):
                dve.wait_ge(A0.filled, A0.count("values", s))
                v.tensor_tensor(vs[q][:], A0.tile[0:TB, :].rearrange("p (k d) -> p k d", k=BLK),
                                bv[:, None, :].broadcast_to([TB, BLK, D]), ALU.add).then_inc(A0.drained, 1)

            def leaky(s, n):
                dve.wait_ge(S.drained, S.count(f"S{n}", s))
                t = pr[n % 2]
                v.scalar_tensor_tensor(out=t[:], in0=t[:], scalar=SLOPE, in1=t[:], op0=ALU.mult,
                                       op1=ALU.max).then_inc(leaky_ready, 1)
                dve.wait_ge(leaky_ready, UNITS * s + n + 1)
                v.tensor_reduce(nmx[n % 2][:], t[:], AX_X, ALU.max, negate=True).then_inc(nmx_ready, 1)

            def attended(s, n):
                k, h0 = n // 2, HU * (n % 2)
                base = 2 * (UNITS * s + n)
                if n > 0:
                    dve.wait_ge(M.drained, M.count(f"AV{n - 1}", s))
                elif not (isinstance(s, int) and s == 0):
                    dve.wait_ge(M.drained, M.count(f"AV{UNITS - 1}", s - 1))
                dve.wait_ge(pr_ready, UNITS * s + n + 1)
                v.reciprocal(rg[:], sums[n % 2][:]).then_inc(av_step, 1)
                dve.wait_ge(av_step, base + 1)
                v.tensor_scalar(rg[:], rg[:], gam[:], None, ALU.mult).then_inc(av_step, 1)
                dve.wait_ge(av_step, base + 2)
                dve.wait_ge(M.filled, M.count(f"AV{n}", s))
                v.tensor_tensor(att[:, k, h0 * DV:(h0 + HU) * DV].rearrange("p (h d) -> p h d", h=HU),
                                M.tile[0:TB, 0:HU * DV].rearrange("p (h d) -> p h d", h=HU),
                                rg[:].rearrange("p (h o) -> p h o", o=1).broadcast_to([TB, HU, DV]),
                                ALU.mult).then_inc(M.drained, 1)

            def gate_part(s, start):
                n = [GSTEPS * s + start]

                def then(ins):
                    ins.then_inc(gate_step, 1)
                    n[0] = n[0] + 1
                    dve.wait_ge(gate_step, n[0])

                def wide(i):
                    return gs[:, i, :].rearrange("p (k o) -> p k o", o=1).broadcast_to([TB, BLK, EXPERTS])

                if start == 0:
                    dve.wait_ge(M.filled, M.count("gate", s))
                    v.tensor_tensor(gl[:], M.tile[0:TB, 0:BLK * EXPERTS].rearrange("p (k e) -> p k e", k=BLK),
                                    bg[:], ALU.add).then_inc(M.drained, 1)
                    dve.wait_ge(M.drained, M.count("gate", s))
                    then(v.tensor_reduce(gs[:, 0, :], gl[:], AX_X, ALU.max))
                    then(v.tensor_tensor(gl[:], gl[:], wide(0), ALU.subtract))
                    return
                dve.wait_ge(gate_exp, s + 1)
                then(v.tensor_reduce(gs[:, 1, :], gl[:], AX_X, ALU.add))
                then(v.reciprocal(gs[:, 1, :], gs[:, 1, :]))
                then(v.tensor_tensor(gl[:], gl[:], wide(1), ALU.mult))
                then(v.tensor_reduce(gs[:, 2, :], gl[:], AX_X, ALU.max))
                for i, (src, oh) in enumerate(((gl, oh1), (g2, oh2))):
                    then(v.tensor_tensor(oh[:], src[:], wide(2 + 2 * i), ALU.is_equal))
                    then(v.tensor_tensor(oh[:], oh[:], rk[:], ALU.mult))
                    then(v.tensor_reduce(gs[:, 3, :], oh[:], AX_X, ALU.max))
                    then(v.tensor_tensor(oh[:], rk[:], wide(3), ALU.is_equal))
                    if i == 0:
                        then(v.scalar_tensor_tensor(out=g2[:], in0=oh[:], scalar=-2.0, in1=gl[:], op0=ALU.mult,
                                                    op1=ALU.add))
                        then(v.tensor_reduce(gs[:, 4, :], g2[:], AX_X, ALU.max))
                v.tensor_tensor(oh1[:], oh1[:], oh2[:], ALU.add)
                then(v.tensor_tensor(gs[:, 5, :], gs[:, 2, :], gs[:, 4, :], ALU.add))
                v.tensor_tensor(gw[:], oh1[:], gl[:], ALU.mult)
                then(v.reciprocal(gs[:, 5, :], gs[:, 5, :]))
                v.tensor_tensor(gw[:], gw[:], wide(5), ALU.mult).then_inc(gate_step, 1)

            def add_pair(s, m):
                pair, k = m // 2, m % 2
                bank = PAIR_BANK[m]
                if m == 0:
                    dve.wait_ge(gate_step, GSTEPS * (s + 1))
                    after(dve, normed["moe"], s)
                dve.wait_ge(bank.filled, bank.count(f"pair{m}", s))
                for e in range(2):
                    if e == 1:
                        dve.wait_ge(moe_step, PAIRS * s + m + 1)
                    elif m >= 2:
                        dve.wait_ge(PAIR_BANK[m - 2].drained, PAIR_BANK[m - 2].count(f"pair{m - 2}", s))
                    src = h3 if m < 2 and e == 0 else acc
                    v.scalar_tensor_tensor(out=acc[:, k, :], in0=bank.tile[0:TB, e * D:(e + 1) * D],
                                           scalar=gw[:, k, 2 * pair + e:2 * pair + e + 1], in1=src[:, k, :],
                                           op0=ALU.mult, op1=ALU.add).then_inc(bank.drained if e else moe_step, 1)

            def add_biases(s):
                dve.wait_ge(F0.filled, F0.count("be", s))
                last = PAIR_BANK[PAIRS - 1]
                dve.wait_ge(last.drained, last.count(f"pair{PAIRS - 1}", s))
                v.tensor_tensor(acc[:], F0.tile[0:TB, :].rearrange("p (k d) -> p k d", k=BLK), acc[:],
                                ALU.add).then_inc(F0.drained, 1)

            def step(b, par):
                for g in range(GROUPS):
                    def at(slot):
                        return live(b, par, g, slot)

                    for s, q in at(AT_TOP2):
                        gate_part(s, GIN)
                    for s, q in at(AT_HEADS):
                        heads(s)
                    for s, q in at(AT_FFN):
                        ffn_sum(s)
                    for s, q in at(AT_SPLIT):
                        split(s)
                    for n in range(UNITS):
                        for s, q in at(AT_AV[n] + 1):
                            attended(s, n)
                    for s, q in at(AT_ATT):
                        dve.wait_ge(M.drained, M.count(f"AV{UNITS - 1}", s))
                        v.scalar_tensor_tensor(out=att[:], in0=h2[q][:], scalar=2.0, in1=att[:], op0=ALU.mult,
                                               op1=ALU.add).then_inc(att_sum, 1)
                        dve.wait_ge(att_sum, s + 1)
                        moments(s, "att", lambda k: att[:, k, :])
                    for s, q in at(AT_BE_OUT):
                        add_biases(s)
                    for s, q in at(AT_OUT_NORM):
                        normalise(s, "out", lambda k: A0.tile[0:TB, k * D:(k + 1) * D], h1, A0.drained)
                    for s, q in at(AT_VALUES_OUT):
                        add_value_bias(s, q)
                    for h in range(HALVES):
                        for s, q in at(AT_REORDER[h]):
                            reorder(s, h)
                    for s, q in at(AT_STEP):
                        step_size(s, q)
                    for s, q in at(AT_GATE_X):
                        gate_x(s)
                    for s, q in at(AT_PAIR[0] + 1):
                        add_pair(s, 0)
                    for k in FOLDED:
                        for s, q in at(k + 2):
                            fold_states(s, k)
                    for m in range(1, PAIRS):
                        for s, q in at(AT_PAIR[m] + 1):
                            add_pair(s, m)
                    for s, q in at(AT_MIX):
                        token_mix(s)
                    for s, q in at(AT_KEEP):
                        if not (isinstance(s, int) and s < 2):
                            dve.wait_ge(A0.filled, A0.count("out", s - 2))
                        v.tensor_copy(hK[q][:], hT[q][:]).then_inc(h_kept, 1)
                    for s, q in at(AT_Z_OUT):
                        gate_z(s)
                    for s, q in at(AT_FFN_NORM):
                        normalise(s, "ffn", lambda k: rs[:, k, :], h2[q], normed["ffn"])
                    for k in range(GROUPS):
                        for s, q in at(k):
                            scan_group(s, k)
                    for s, q in at(AT_ATT_NORM):
                        normalise(s, "att", lambda k: att[:, k, :], h3, normed["att"])
                    for s, q in at(AT_Y_NORM):
                        normalise(s, "y", lambda k: ysb[:, k, :], ysb, normed["y"])
                    for s, q in at(AT_GATE_IN):
                        gate_part(s, 0)
                    for n in range(UNITS):
                        for s, q in at(AT_SCORES[n] + 2):
                            leaky(s, n)
                    for t, which in AT_TAPS.items():
                        for s, q in at(t):
                            taps(s, which)
                    for s, q in at(AT_FFN_STATS):
                        dve.wait_ge(ffn_sum_done, s + 1)
                        moments(s, "ffn", lambda k: rs[:, k, :])
                    for s, q in at(AT_MOE_STATS):
                        dve.wait_ge(F0.drained, F0.count("be", s))
                        moments(s, "moe", lambda k: acc[:, k, :])
                    for s, q in at(AT_Y_STATS):
                        dve.wait_ge(y_drained, IC * (s + 1))
                        moments(s, "y", lambda k: ysb[:, k, :])
                    for k in DVE_INPUTS:
                        for s, q in at(k - 1):
                            inputs(s, q, k)
                    for s, q in at(AT_MOE_NORM):
                        after(dve, out_landed, 16 * s)
                        normalise(s, "moe", lambda k: acc[:, k, :], ob, normed["moe"])
                    for s, q in at(AT_OUT_STATS):
                        dve.wait_ge(A0.filled, A0.count("out", s))
                        moments(s, "out", lambda k: A0.tile[0:TB, k * D:(k + 1) * D])

            dve.wait_ge(w_landed, W_ALL)
            for t in (cw, cb, lng, lnb, wv):
                v.tensor_scalar(t[:], t[:], 0.5, None, ALU.mult).then_inc(const_ready, 1)
            v.tensor_scalar(omr[:], mur[:], -1.0, 1.0, ALU.mult, ALU.add).then_inc(const_ready, 1)
            v.tensor_scalar(omk[:], muk[:], -1.0, 1.0, ALU.mult, ALU.add).then_inc(const_ready, 1)
            v.tensor_copy(sel[:], selF[:]).then_inc(const_ready, 1)
            dve.wait_ge(nega_exp, 1)
            v.tensor_scalar(negA[:], negA[:], -1.0, None, ALU.mult).then_inc(const_ready, 1)
            dve.wait_ge(const_ready, CONSTS)
            dve.wait_ge(zeros_ready, 3)
            schedule(dve, step)


_INS = ["x", "w_tok", "b_tok", "w_in", "conv_w", "conv_b", "w_xproj", "a_log", "d_par", "dt_w", "dt_b", "w_out",
        "ln_g", "ln_b", "w_r", "w_k", "w_v", "mu_r", "mu_k", "w_qk", "b_q", "b_k", "w_vv", "b_v", "gamma",
        "w_g", "b_g", "w_e", "b_e", "ident", "select", "split_masks", "head_mask", "rank"]


def kernel(**inputs):
    import numpy as np
    import concourse.bacc as _bacc
    from concourse import mybir as _mybir
    from concourse.bass_utils import run_bass_kernel_spmd as _run

    a = {k: np.asarray(v) for k, v in inputs.items()}

    def cols(w):
        return w.reshape(w.shape[0] // P, P, *w.shape[1:]).swapaxes(0, 1)

    f = np.float32
    rows = np.arange(STK)
    laid = {
        "x": a["x"].reshape(IMAGES * CROWS, PATCH * WIDTH),
        "w_tok": cols(a["L0_tok_W"].T),
        "b_tok": cols(a["L0_tok_b"]),
        "w_in": cols(a["L0_attn_in_proj_w"].T),
        "conv_w": cols(a["L0_attn_conv_w"]),
        "conv_b": cols(a["L0_attn_conv_b"]),
        "w_xproj": cols(np.tile(a["L0_attn_x_proj_w"].T, (1, PARTS))),
        "a_log": cols(a["L0_attn_A_log"]),
        "d_par": cols(a["L0_attn_D_param"]),
        "dt_w": cols(a["L0_attn_dt_w"][:, 0]),
        "dt_b": cols(a["L0_attn_dt_b"]),
        "w_out": cols(a["L0_attn_out_w"].T),
        "ln_g": cols(a["L0_attn_ln_g"]),
        "ln_b": cols(a["L0_attn_ln_b"]),
        "w_r": cols(a["L0_ffn_W_r"].T),
        "w_k": cols(a["L0_ffn_W_k"].T),
        "w_v": cols(a["L0_ffn_W_v"].T),
        "mu_r": cols(a["L0_ffn_mu_r"]),
        "mu_k": cols(a["L0_ffn_mu_k"]),
        "w_qk": cols(np.concatenate([a["L1_attn_Wq"], a["L1_attn_Wk"]]).T),
        "b_q": a["L1_attn_bq"].reshape(QK, 1),
        "b_k": a["L1_attn_bk"].reshape(QK, 1),
        "w_vv": cols(a["L1_attn_Wv"].T),
        "b_v": np.tile(a["L1_attn_bv"], (TB, 1)),
        "gamma": np.tile(a["L1_attn_gamma"], (TB, 1)),
        "w_g": cols(a["L1_ffn_Wg"]),
        "b_g": np.tile(a["L1_ffn_bg"], (TB, BLK, 1)),
        "w_e": cols(a["L1_ffn_We"].transpose(2, 0, 1).reshape(D, EXPERTS * D)),
        "b_e": a["L1_ffn_be"],
        "ident": np.eye(P, dtype=f),
        "select": (rows[:, None] % PROJ == np.arange(PROJ)[None, :]).astype(f),
        "split_masks": -np.stack([rows >= PROJ, rows >= 2 * PROJ], 1).astype(f),
        "head_mask": ((np.arange(QK)[:, None] // (QK // HEADS)) == np.arange(HEADS)[None, :]).astype(f)
        * f((QK // HEADS) ** -0.5),
        "rank": np.tile(np.arange(EXPERTS, 0, -1, dtype=f), (TB, BLK, 1)),
    }
    nc = _bacc.Bacc("TRN2", target_bir_lowering=False, num_devices=1)
    arrays, args = {}, []
    for name in _INS:
        w = np.ascontiguousarray(laid[name])
        arrays[f"in_{name}"] = w
        args.append(nc.dram_tensor(f"in_{name}", w.shape, _mybir.dt.from_np(w.dtype), kind="ExternalInput").ap())
    out = nc.dram_tensor("out_0", (IMAGES * T, D), F32, kind="ExternalOutput").ap()
    vit_tower(nc, *args, out)
    r = _run(nc, [arrays], core_ids=[0])
    return r.results[0]["out_0"].reshape(IMAGES, T, D)
```
